# Optimizing a Trainium2 kernel written in Bass

```python
import numpy as np
import jax
import jax.numpy as jnp

def _softmax(x, axis=-1):
    return jax.nn.softmax(x, axis=axis)

def _gelu(x):
    return jax.nn.gelu(x, approximate=True)

def _silu(x):
    return jax.nn.silu(x)

def _sigmoid(x):
    return jax.nn.sigmoid(x)

def _layernorm(x, axis=-1, eps=1e-05):
    m = jnp.mean(x, axis=axis, keepdims=True)
    v = jnp.var(x, axis=axis, keepdims=True)
    return (x - m) / jnp.sqrt(v + eps)

def _scatter_add(tgt, idx, src, axis=0):
    return tgt.at[idx].add(src)

def _segment_sum(src, seg, n):
    return jax.ops.segment_sum(src, seg, n)
kernel_name = 'mk_cond_seq_d2_seqx_r4_374a93'

def setup_inputs(seed: int=0):
    np.random.seed(seed)
    _w = jnp.asarray

    def _rec_inputs():
        import jax
        import jax.numpy as jnp
        _rk = jax.random.key(seed)
        x = -0.0002928 + 1 * jax.random.normal(jax.random.fold_in(_rk, 1), (16, 256, 256), jnp.float32)
        _lenS = 256 - jax.random.randint(jax.random.fold_in(_rk, 7), (16,), 0, max(1, 256 // 4) + 1, jnp.int32)
        _lenS2 = 256 - jax.random.randint(jax.random.fold_in(_rk, 8), (16,), 0, max(1, 256 // 4) + 1, jnp.int32)
        cond_1024 = 0.0061147 + 1.02565 * jax.random.normal(jax.random.fold_in(_rk, 11), (16, 256), jnp.float32)
        _validS = jnp.arange(256)[None, :] < _lenS[:, None]
        _validS2 = jnp.arange(256)[None, :] < _lenS2[:, None]
        _causal = jnp.tril(jnp.ones((256, 256), dtype=bool))
        mask_BxS_bf0 = jnp.logical_not(jnp.ones((16, 256), dtype=bool))
        return (x, cond_1024, mask_BxS_bf0)
    x, cond_1024, mask_BxS_bf0 = _rec_inputs()

    def _L0_cond_setup():
        import jax, jax.numpy as jnp
        import numpy as np
        D = 256
        H = 16
        HD = 4 * D
        B, T = (4, 256)
        EPS = 1e-05

        def _layernorm(x, g, b):
            mu = jnp.mean(x, axis=-1, keepdims=True)
            var = jnp.mean(jnp.square(x - mu), axis=-1, keepdims=True)
            return (x - mu) * jax.lax.rsqrt(var + EPS) * g + b

        def _attention(x, Wqkv, Wproj, bproj):
            b, t, c = x.shape
            hd = c // H
            qkv = (x @ Wqkv).reshape(b, t, 3, H, hd).transpose(2, 0, 3, 1, 4)
            q, k, v = (qkv[0], qkv[1], qkv[2])
            scale = hd ** (-0.5)
            scores = jnp.einsum('bhqd,bhkd->bhqk', q, k) * scale
            causal = jnp.tril(jnp.ones((t, t), bool))
            scores = jnp.where(causal, scores, -jnp.inf)
            attn = jax.nn.softmax(scores, axis=-1)
            out = jnp.einsum('bhqk,bhkd->bhqd', attn, v)
            out = out.transpose(0, 2, 1, 3).reshape(b, t, c)
            return out @ Wproj + bproj
        key = jax.random.key(seed)
        ks = jax.random.split(key, 12)
        s = 0.02
        return {'x': jax.random.normal(ks[0], (B, T, D), jnp.float32), 'condition': jax.random.normal(ks[1], (B, D), jnp.float32), 'Wqkv': jax.random.normal(ks[2], (D, 3 * D), jnp.float32) * s, 'Wproj': jax.random.normal(ks[3], (D, D), jnp.float32) * s, 'bproj': jnp.zeros((D,), jnp.float32), 'W1': jax.random.normal(ks[4], (D, HD), jnp.float32) * s, 'b1': jnp.zeros((HD,), jnp.float32), 'W2': jax.random.normal(ks[5], (HD, D), jnp.float32) * s, 'b2': jnp.zeros((D,), jnp.float32), 'g1': jnp.ones((D,), jnp.float32), 'be1': jnp.zeros((D,), jnp.float32), 'g2': jnp.ones((D,), jnp.float32), 'be2': jnp.zeros((D,), jnp.float32), 'Wada': jax.random.normal(ks[6], (D, 6 * D), jnp.float32) * s, 'bada': jax.random.normal(ks[7], (6 * D,), jnp.float32) * s}
    _L0_cond_all = _L0_cond_setup()
    _L0_cond_in = {k: v for k, v in _L0_cond_all.items() if k in ('Wqkv', 'Wproj', 'bproj', 'W1', 'b1', 'W2', 'b2', 'g1', 'be1', 'g2', 'be2', 'Wada', 'bada')}
    del _L0_cond_all

    def _L1_cond_setup():
        import math
        import jax, jax.numpy as jnp
        import numpy as np
        H = 256
        NH = 16
        HD = H // NH
        CD = 256
        MLP = 1024
        EPS = 1e-05

        def _layernorm(x):
            mu = jnp.mean(x, axis=-1, keepdims=True)
            var = jnp.var(x, axis=-1, keepdims=True)
            return (x - mu) * jax.lax.rsqrt(var + EPS)

        def _adaln(x, cond, W, b):
            ss = cond @ W.T + b
            scale, shift = jnp.split(ss, 2, axis=-1)
            return _layernorm(x) * (1.0 + scale[:, None, :]) + shift[:, None, :]
        key = jax.random.key(seed)
        ks = jax.random.split(key, 16)
        s = 0.02
        inp = {'x': jax.random.normal(ks[0], (2, 512, H), jnp.float32), 'cond': jax.random.normal(ks[1], (2, CD), jnp.float32), 'key_padding_mask': jnp.zeros((2, 512), dtype=bool), 'w_adaln1': jax.random.normal(ks[2], (2 * H, CD), jnp.float32) * s, 'b_adaln1': jnp.zeros((2 * H,), jnp.float32), 'w_adaln2': jax.random.normal(ks[3], (2 * H, CD), jnp.float32) * s, 'b_adaln2': jnp.zeros((2 * H,), jnp.float32), 'wq': jax.random.normal(ks[4], (H, H), jnp.float32) * s, 'bq': jnp.zeros((H,), jnp.float32), 'wk': jax.random.normal(ks[5], (H, H), jnp.float32) * s, 'bk': jnp.zeros((H,), jnp.float32), 'wv': jax.random.normal(ks[6], (H, H), jnp.float32) * s, 'bv': jnp.zeros((H,), jnp.float32), 'wo': jax.random.normal(ks[7], (H, H), jnp.float32) * s, 'bo': jnp.zeros((H,), jnp.float32), 'w1': jax.random.normal(ks[8], (MLP, H), jnp.float32) * s, 'b1': jnp.zeros((MLP,), jnp.float32), 'w2': jax.random.normal(ks[9], (H, MLP), jnp.float32) * s, 'b2': jnp.zeros((H,), jnp.float32)}
        return inp
    _L1_cond_all = _L1_cond_setup()
    _L1_cond_in = {k: v for k, v in _L1_cond_all.items() if k in ('w_adaln1', 'b_adaln1', 'w_adaln2', 'b_adaln2', 'wq', 'bq', 'wk', 'bk', 'wv', 'bv', 'wo', 'bo', 'w1', 'b1', 'w2', 'b2')}
    del _L1_cond_all
    return {'x': x, 'cond_1024': cond_1024, 'mask_BxS_bf0': mask_BxS_bf0, 'L0_cond_Wqkv': _L0_cond_in['Wqkv'], 'L0_cond_Wproj': _L0_cond_in['Wproj'], 'L0_cond_bproj': _L0_cond_in['bproj'], 'L0_cond_W1': _L0_cond_in['W1'], 'L0_cond_b1': _L0_cond_in['b1'], 'L0_cond_W2': _L0_cond_in['W2'], 'L0_cond_b2': _L0_cond_in['b2'], 'L0_cond_g1': _L0_cond_in['g1'], 'L0_cond_be1': _L0_cond_in['be1'], 'L0_cond_g2': _L0_cond_in['g2'], 'L0_cond_be2': _L0_cond_in['be2'], 'L0_cond_Wada': _L0_cond_in['Wada'], 'L0_cond_bada': _L0_cond_in['bada'], 'L1_cond_w_adaln1': _L1_cond_in['w_adaln1'], 'L1_cond_b_adaln1': _L1_cond_in['b_adaln1'], 'L1_cond_w_adaln2': _L1_cond_in['w_adaln2'], 'L1_cond_b_adaln2': _L1_cond_in['b_adaln2'], 'L1_cond_wq': _L1_cond_in['wq'], 'L1_cond_bq': _L1_cond_in['bq'], 'L1_cond_wk': _L1_cond_in['wk'], 'L1_cond_bk': _L1_cond_in['bk'], 'L1_cond_wv': _L1_cond_in['wv'], 'L1_cond_bv': _L1_cond_in['bv'], 'L1_cond_wo': _L1_cond_in['wo'], 'L1_cond_bo': _L1_cond_in['bo'], 'L1_cond_w1': _L1_cond_in['w1'], 'L1_cond_b1': _L1_cond_in['b1'], 'L1_cond_w2': _L1_cond_in['w2'], 'L1_cond_b2': _L1_cond_in['b2']}

def reference(x, cond_1024, mask_BxS_bf0, L0_cond_Wqkv, L0_cond_Wproj, L0_cond_bproj, L0_cond_W1, L0_cond_b1, L0_cond_W2, L0_cond_b2, L0_cond_g1, L0_cond_be1, L0_cond_g2, L0_cond_be2, L0_cond_Wada, L0_cond_bada, L1_cond_w_adaln1, L1_cond_b_adaln1, L1_cond_w_adaln2, L1_cond_b_adaln2, L1_cond_wq, L1_cond_bq, L1_cond_wk, L1_cond_bk, L1_cond_wv, L1_cond_bv, L1_cond_wo, L1_cond_bo, L1_cond_w1, L1_cond_b1, L1_cond_w2, L1_cond_b2):
    import jax
    import jax.numpy as jnp

    def _L0_cond_ref(x, condition, Wqkv, Wproj, bproj, W1, b1, W2, b2, g1, be1, g2, be2, Wada, bada):
        import jax, jax.numpy as jnp
        import numpy as np
        D = 256
        H = 16
        HD = 4 * D
        B, T = (4, 256)
        EPS = 1e-05

        def _layernorm(x, g, b):
            mu = jnp.mean(x, axis=-1, keepdims=True)
            var = jnp.mean(jnp.square(x - mu), axis=-1, keepdims=True)
            return (x - mu) * jax.lax.rsqrt(var + EPS) * g + b

        def _attention(x, Wqkv, Wproj, bproj):
            b, t, c = x.shape
            hd = c // H
            qkv = (x @ Wqkv).reshape(b, t, 3, H, hd).transpose(2, 0, 3, 1, 4)
            q, k, v = (qkv[0], qkv[1], qkv[2])
            scale = hd ** (-0.5)
            scores = jnp.einsum('bhqd,bhkd->bhqk', q, k) * scale
            causal = jnp.tril(jnp.ones((t, t), bool))
            scores = jnp.where(causal, scores, -jnp.inf)
            attn = jax.nn.softmax(scores, axis=-1)
            out = jnp.einsum('bhqk,bhkd->bhqd', attn, v)
            out = out.transpose(0, 2, 1, 3).reshape(b, t, c)
            return out @ Wproj + bproj
        mod = jax.nn.silu(condition) @ Wada + bada
        sh_a, sc_a, gt_a, sh_m, sc_m, gt_m = jnp.split(mod, 6, axis=1)
        xn = _layernorm(x, g1, be1)
        xm = xn * (1.0 + sc_a[:, None, :]) + sh_a[:, None, :]
        x = x + gt_a[:, None, :] * _attention(xm, Wqkv, Wproj, bproj)
        xn = _layernorm(x, g2, be2)
        xm = xn * (1.0 + sc_m[:, None, :]) + sh_m[:, None, :]
        h = jax.nn.gelu(xm @ W1 + b1, approximate=False)
        x = x + gt_m[:, None, :] * (h @ W2 + b2)
        return x

    def _L1_cond_ref(x, cond, key_padding_mask, w_adaln1, b_adaln1, w_adaln2, b_adaln2, wq, bq, wk, bk, wv, bv, wo, bo, w1, b1, w2, b2):
        import math
        import jax, jax.numpy as jnp
        import numpy as np
        H = 256
        NH = 16
        HD = H // NH
        CD = 256
        MLP = 1024
        EPS = 1e-05

        def _layernorm(x):
            mu = jnp.mean(x, axis=-1, keepdims=True)
            var = jnp.var(x, axis=-1, keepdims=True)
            return (x - mu) * jax.lax.rsqrt(var + EPS)

        def _adaln(x, cond, W, b):
            ss = cond @ W.T + b
            scale, shift = jnp.split(ss, 2, axis=-1)
            return _layernorm(x) * (1.0 + scale[:, None, :]) + shift[:, None, :]
        B, L, D = x.shape
        normed = _adaln(x, cond, w_adaln1, b_adaln1)
        q = (normed @ wq.T + bq).reshape(B, L, NH, HD)
        k = (normed @ wk.T + bk).reshape(B, L, NH, HD)
        v = (normed @ wv.T + bv).reshape(B, L, NH, HD)
        scale = math.sqrt(HD)
        scores = jnp.einsum('blhd,bmhd->bhlm', q, k) / scale
        scores = jnp.where(key_padding_mask[:, None, None, :], -jnp.inf, scores)
        attn = jax.nn.softmax(scores, axis=-1)
        attn_out = jnp.einsum('bhlm,bmhd->blhd', attn, v).reshape(B, L, D)
        x = x + attn_out @ wo.T + bo
        normed = _adaln(x, cond, w_adaln2, b_adaln2)
        h = jax.nn.gelu(normed @ w1.T + b1, approximate=False)
        x = x + h @ w2.T + b2
        return x
    x = _L0_cond_ref(x, cond_1024, L0_cond_Wqkv, L0_cond_Wproj, L0_cond_bproj, L0_cond_W1, L0_cond_b1, L0_cond_W2, L0_cond_b2, L0_cond_g1, L0_cond_be1, L0_cond_g2, L0_cond_be2, L0_cond_Wada, L0_cond_bada)
    x = _L1_cond_ref(x, cond_1024, mask_BxS_bf0, L1_cond_w_adaln1, L1_cond_b_adaln1, L1_cond_w_adaln2, L1_cond_b_adaln2, L1_cond_wq, L1_cond_bq, L1_cond_wk, L1_cond_bk, L1_cond_wv, L1_cond_bv, L1_cond_wo, L1_cond_bo, L1_cond_w1, L1_cond_b1, L1_cond_w2, L1_cond_b2)
    return x

_drawn_inputs = setup_inputs


def setup_inputs(seed=0):
    import zlib

    import numpy as np

    out = dict(_drawn_inputs(seed))
    spreads = {'L0_cond_bproj': (0.0, 0.394),
     'L0_cond_b1': (0.0, 0.8),
     'L0_cond_b2': (0.0, 0.447),
     'L0_cond_g1': (1.0, 0.6),
     'L0_cond_be1': (0.0, 0.8),
     'L0_cond_g2': (1.0, 0.6),
     'L0_cond_be2': (0.0, 2.0),
     'L1_cond_b_adaln1': (0.0, 0.8),
     'L1_cond_b_adaln2': (0.0, 1.384),
     'L1_cond_bq': (0.0, 2.0),
     'L1_cond_bk': (0.0, 2.0),
     'L1_cond_bv': (0.0, 0.738),
     'L1_cond_bo': (0.0, 0.1),
     'L1_cond_b1': (0.0, 0.593),
     'L1_cond_b2': (0.0, 0.1)}
    factors = {'L0_cond_Wqkv': 8.0,
     'L0_cond_Wproj': 8.0,
     'L0_cond_bada': 8.0,
     'L1_cond_wq': 8.0,
     'L1_cond_wk': 8.0,
     'L0_cond_W1': 2.9,
     'L1_cond_w_adaln2': 2.928}
    for name, (base, spread) in spreads.items():
        noise = np.random.default_rng([zlib.crc32(name.encode()), seed]).standard_normal(out[name].shape)
        drawn = base * np.exp(spread * noise) if base else spread * noise
        out[name] = jnp.asarray(drawn.astype(out[name].dtype))
    for name, factor in factors.items():
        out[name] = (out[name] * factor).astype(out[name].dtype)
    return out
```

```python
import concourse.bass as bass
from concourse import mybir
from contextlib import ExitStack

LAYERS, B, T, D = 2, 16, 256, 256
H, HD = 16, 16
F = 4 * D
P = 128
NF, NM, NT = D // P, F // P, T // P
EPS = 1e-5
SCALE = HD ** -0.5
BIG = -1e30
GROUP = 4
NG = H // GROUP
SLOTS = H // 2
SBUFS = 4
LAG = 6
ROW_MASK, ROW_MAX, ROWS = 3 * HD, 3 * HD + 1, 3 * HD + 3

COLS, _at = {}, 0
for _name, _n in [("g1", NF), ("be1", NF), ("g2", NF), ("be2", NF), ("bproj", NF), ("b2_0", NF), ("b1_0", NM),
                  ("bada", 6 * NF), ("bada1", 4 * NF), ("bqk", 2 * NF), ("bv", NF), ("bo", NF), ("b1_1", NM),
                  ("b2_1", NF)]:
    COLS[_name] = (_at, _n)
    _at += _n
NCOLS = _at
A1, B1, G1, GB1, A2, B2, G2, GB2 = range(8)


class Step:

    def __init__(self, const, reg=None, stride=0):
        self.const, self.reg, self.stride = const, reg, stride

    def __sub__(self, k):
        return Step(self.const - k, self.reg, self.stride)

    def within(self, n):
        return self.reg is not None or 0 <= self.const < n

    def mod(self, m):
        return self.const % m

    def half(self):
        return Step(self.const // 2, self.reg, self.stride // 2)

    def count(self, each, plus=0):
        v = self.const * each + plus
        if self.reg is not None:
            return self.reg * (self.stride * each) + v
        return v if v > 0 else None


def wait(eng, sem, value):
    if value is not None:
        eng.wait_ge(sem, value)


def wait_apart(eng, sem, value, passed):
    if value is not None:
        eng.wait_ge(sem, value)
        eng.sem_inc(passed, 1)


def steps(eng, n, stages, unroll):
    last = n + stages - 1
    first = stages - 1
    turns = (n - first) // unroll
    for t in range(first):
        yield Step(t)
    with eng.Fori(0, turns) as i:
        for u in range(unroll):
            yield Step(first + u, i, unroll)
    for t in range(first + turns * unroll, last):
        yield Step(t)


def head_place(h):
    pair, parity = h // 2, h % 2
    tile, i = pair // 4, pair % 4
    return 64 * parity, i * NF + tile


def build(nc, x_in, cond_in, mask_in, wqkv_in, wproj_in, w1_in, w2_in, ada0_in, ada1_in, cols_in, ident_in,
          tri_in, out):
    fp32, f32r, bf16 = mybir.dt.float32, mybir.dt.float32r, mybir.dt.bfloat16
    ALU, ACT, AX = mybir.AluOpType, mybir.ActivationFunctionType, mybir.AxisListType

    with ExitStack() as ctx:
        def sb(name, shape, dt=fp32):
            return ctx.enter_context(nc.sbuf_tensor(name, shape, dt))

        def bank(name):
            return ctx.enter_context(nc.psum_tensor(name, [P, 512], fp32))

        def sem(name):
            return ctx.enter_context(nc.semaphore(name))

        x_sb = sb("x_sb", [P, B * NT * D])
        wqkv = sb("wqkv", [P, LAYERS, NF, 3 * D])
        wproj = sb("wproj", [P, LAYERS, NF, D])
        w1 = sb("w1", [P, NF, F])
        w2 = sb("w2", [P, NM, D])
        cols = sb("cols", [P, NCOLS])
        ident = sb("ident", [P, P])
        ident16 = sb("ident16", [P, P], bf16)
        tri = sb("tri", [P, P])
        tri16 = sb("tri16", [P, P], bf16)
        cond = sb("cond", [P, NF, B])
        silu = sb("silu", [P, NF, B])
        sig = sb("sig", [P, NF, B])
        mod0 = sb("mod0", [P, 6 * NF, B])
        mod1 = sb("mod1", [P, 4 * NF, B])
        bfold = sb("bfold", [P, NF])
        table = [sb(f"table{l}", [P, 8 * NF * B]) for l in range(LAYERS)]
        mask_int = sb("mask_int", [B, T], mybir.dt.int32)
        maskf = sb("maskf", [B, T], f32r)
        q_stack = sb("q_stack", [P, SBUFS, SLOTS, T], f32r)
        k_stack = sb("k_stack", [P, SBUFS, SLOTS, T], f32r)
        v_sb = sb("v_sb", [P, SBUFS, NT, H, 32])
        probs = sb("probs", [P, 8, 512])
        stats = sb("stats", [P, 2, NT, 6])
        mv = sb("mv", [P, 2, NT, 2])
        rstd = sb("rstd", [P, 2, NT])
        xn = sb("xn", [P, 2, NT, D])
        xmT = sb("xmT", [P, 2, NF, T])
        q_split = sb("q_split", [P, 2, NF, T], f32r)
        k_split = sb("k_split", [P, 2, NF, T], f32r)
        maxima = sb("maxima", [P, 2, H, 3])
        negmax = sb("negmax", [P, 2, NT, 2, 2, SLOTS], f32r)
        negmaxT = sb("negmaxT", [32, 2, T], f32r)
        o_sb = sb("o_sb", [P, 2, NG, T])
        rsum = sb("rsum", [P, 2, H])
        attn = sb("attn", [P, 2, NT, D])
        attnT = sb("attnT", [P, NF, T])
        y_sb = sb("y_sb", [P, NF, T])

        ada0 = probs[:].rearrange("p a n -> p (a n)")[:, 0:NF * 6 * D].rearrange("p (f n) -> p f n", f=NF)
        ada1 = o_sb[:].rearrange("p a g n -> p (a g n)").rearrange("p (f n) -> p f n", f=NF)
        hT = probs
        CH = 2 * T
        CT = CH // P
        xn_m = o_sb[:].rearrange("p a g n -> p (a g n)").rearrange("p (a t n) -> p a t n", a=2, t=CT)
        xmT_m = v_sb[:].rearrange("p a t h n -> p (a t h n)")[:, 0:2 * NF * CH]\
            .rearrange("p (a f n) -> p a f n", a=2, f=NF)
        y_m = v_sb[:].rearrange("p a t h n -> p (a t h n)")[:, 2 * NF * CH:4 * NF * CH]\
            .rearrange("p (a f n) -> p a f n", a=2, f=NF)
        stats_m = sb("stats_m", [P, 2, CT, 6])
        mv_m = sb("mv_m", [P, 2, CT, 2])
        rstd_m = sb("rstd_m", [P, 2, CT])
        half_power = sb("half_power", [P, CT])

        q_dram = nc.dram_tensor("q_dram", (2, 2, P, NF * T), fp32, kind="Internal").ap()
        k_dram = nc.dram_tensor("k_dram", (2, 2, P, NF * T), fp32, kind="Internal").ap()
        mask_dram = nc.dram_tensor("mask_dram", (B, T), fp32, kind="Internal").ap()

        s_bank = [bank(f"s_bank{i}") for i in range(2)]
        st_bank = [bank(f"st_bank{i}") for i in range(2)]
        o_bank = [bank(f"o_bank{i}") for i in range(2)]
        g_bank = [bank(f"g_bank{i}") for i in range(2)]

        vec_loaded = sem("vec_loaded")
        x_loaded = [sem(f"x_loaded{i}") for i in range(4)]
        wa_loaded = sem("wa_loaded")
        wm_loaded = sem("wm_loaded")
        ones_set = sem("ones_set")
        rows_set = sem("rows_set")
        vones_set = sem("vones_set")
        chain = sem("chain")
        expneg = sem("expneg")
        silu_ready = sem("silu_ready")
        mods_ready = sem("mods_ready")
        setup_done = sem("setup_done")
        maskf_ready = sem("maskf_ready")
        mask_stored = sem("mask_stored")
        stats_part = sem("stats_part")
        power_set = sem("power_set")
        sp_passed, dve_passed, pool_passed = sem("sp_passed"), sem("dve_passed"), sem("pool_passed")
        var_shifted = sem("var_shifted")
        m_shifted = sem("m_shifted")
        mv_ready = sem("mv_ready")
        rstd_ready = sem("rstd_ready")
        xn_ready = sem("xn_ready")
        xT_ready = sem("xT_ready")
        xmT_ready = sem("xmT_ready")
        q_ready = sem("q_ready")
        k_ready = sem("k_ready")
        v_ready = sem("v_ready")
        q_hi = sem("q_hi")
        k_hi = sem("k_hi")
        q_lo = sem("q_lo")
        k_lo = sem("k_lo")
        v_copied = sem("v_copied")
        q_stored = sem("q_stored")
        k_stored = sem("k_stored")
        stack_loaded = [sem(f"stack_loaded{i}") for i in range(2)]
        mask_loaded = [sem(f"mask_loaded{i}") for i in range(2)]
        max_loaded = [sem(f"max_loaded{i}") for i in range(2)]
        s_ready = sem("s_ready")
        max_done = sem("max_done")
        max_joined = sem("max_joined")
        negmax_hi = sem("negmax_hi")
        negmax_ready = sem("negmax_ready")
        negmaxT_ready = sem("negmaxT_ready")
        negmaxT_copied = sem("negmaxT_copied")
        st_ready = sem("st_ready")
        exp_done = sem("exp_done")
        pv_done = sem("pv_done")
        o_copied = sem("o_copied")
        oT_ready = sem("oT_ready")
        rsum_ready = sem("rsum_ready")
        attn_ready = sem("attn_ready")
        attnT_ready = sem("attnT_ready")
        attnT_copied = sem("attnT_copied")
        proj_ready = sem("proj_ready")
        y_copied = sem("y_copied")
        yT_ready = sem("yT_ready")
        x_added = sem("x_added")
        m_stats = sem("m_stats")
        m_mv = sem("m_mv")
        m_rstd = sem("m_rstd")
        m_xn = sem("m_xn")
        m_xT = sem("m_xT")
        m_xmT = sem("m_xmT")
        m_h = sem("m_h")
        m_gelu = sem("m_gelu")
        m_y = sem("m_y")
        m_ycopied = sem("m_ycopied")
        m_yT = sem("m_yT")
        m_added = sem("m_added")
        out_stored = sem("out_stored")

        block = ctx.enter_context(nc.Block())
        NCH = B * T // CH
        VEC_LOADS, STACK_LOADS = 8, 8

        def tab(layer, kind, f, b):
            at = b.count(1, (kind * NF + f) * B)
            return table[layer][:, bass.ds(0 if at is None else at, 1)]

        def xrows(b, tiles, first=0):
            at = b.count(NT * D, first * D)
            return x_sb[:, bass.ds(0 if at is None else at, tiles * D)]

        def in_layer(layer, b):
            return b - (-B * layer)

        @block.sync
        def _(sp):
            for dst, src in [(ident[:], ident_in), (cols[:], cols_in), (cond[:], cond_in), (mask_int[:], mask_in),
                             (tri[:], tri_in), (ada0[:, 0], ada0_in[:, 0]), (ada0[:, 1], ada0_in[:, 1]),
                             (ada1, ada1_in)]:
                sp.dma_start(dst, src).then_inc(vec_loaded, 16)
            n = B * NT // 4
            xt = x_in.rearrange("(t p) d -> p t d", p=P)
            for i in range(4):
                sp.dma_start(x_sb[:, i * n * D:(i + 1) * n * D].rearrange("p (t d) -> p t d", d=D),
                             xt[:, i * n:(i + 1) * n, :]).then_inc(x_loaded[i], 16)
                if i == 0:
                    for l in range(LAYERS):
                        sp.dma_start(wqkv[:, l], wqkv_in[l]).then_inc(wa_loaded, 16)
                        sp.dma_start(wproj[:, l], wproj_in[l]).then_inc(wa_loaded, 16)
            sp.wait_ge(ones_set, 2)
            ones = q_split[:].rearrange("p a f n -> p (a f n)").bitcast(fp32)
            zeros = k_split[:].rearrange("p a f n -> p (a f n)").bitcast(fp32)
            for p in (0, 64):
                qs = q_stack[:].rearrange("p a s n -> p (a s n)").bitcast(fp32)
                ks = k_stack[:].rearrange("p a s n -> p (a s n)").bitcast(fp32)
                sp.dma_start(qs[p + ROW_MASK:p + ROW_MASK + 1, :], ones[0:8, :]).then_inc(rows_set, 16)
                sp.dma_start(ks[p + ROW_MAX:p + ROW_MAX + 2, :], ones[0:16, :]).then_inc(rows_set, 16)
                sp.dma_start(ks[p + ROW_MASK:p + ROW_MASK + 1, :], zeros[0:8, :]).then_inc(rows_set, 16)
            sp.wait_ge(maskf_ready, 1)
            sp.dma_start(mask_dram, maskf[:].bitcast(fp32)).then_inc(mask_stored, 16)
            sp.dma_start(w1[:], w1_in[0]).then_inc(wm_loaded, 16)
            sp.dma_start(w2[:], w2_in[0]).then_inc(wm_loaded, 16)
            sp.wait_ge(mask_stored, 16)

            def when(sem, value):
                wait_apart(sp, sem, value, sp_passed)

            def step(layer, t):
                c, a = t - 3, t - 1
                if c.within(B):
                    g = in_layer(layer, c)
                    when(negmaxT_copied, g.count(1, 1))
                    for p, first in ((0, 0), (64, 16)):
                        sp.dma_start(q_stack[p + ROW_MAX:p + ROW_MAX + 2, g.mod(SBUFS)].bitcast(fp32),
                                     negmaxT[first:first + 16, g.mod(2)].bitcast(fp32))\
                            .then_inc(max_loaded[g.mod(2)], 16)
                if a.within(B):
                    g = in_layer(layer, a)
                    par = g.mod(2)
                    when(stack_loaded[par], g.half().count(16 * STACK_LOADS))
                    when(q_lo, g.count(1, 1))
                    sp.dma_start(q_dram[par].rearrange("a p n -> p a n"),
                                 q_split[:].bitcast(fp32).rearrange("p a f n -> p a (f n)")).then_inc(q_stored, 16)
                    when(k_lo, g.count(1, 1))
                    sp.dma_start(k_dram[par].rearrange("a p n -> p a n"),
                                 k_split[:].bitcast(fp32).rearrange("p a f n -> p a (f n)")).then_inc(k_stored, 16)
                    when(st_ready, g.count(H, H - SBUFS * H))
                    when(q_stored, g.count(16, 16))
                    for half in (0, 1):
                        src = q_dram[par].rearrange("a (h d i) n -> h a d (i n)", h=2, d=HD)[half]
                        dst = q_stack[64 * half:64 * half + 3 * HD, g.mod(SBUFS)].bitcast(fp32)\
                            .rearrange("p s n -> p (s n)")
                        sp.dma_start(dst[0:2 * HD], src).then_inc(stack_loaded[par], 16)
                        sp.dma_start(dst[2 * HD:3 * HD], src[0]).then_inc(stack_loaded[par], 16)
                    when(k_stored, g.count(16, 16))
                    for half in (0, 1):
                        src = k_dram[par].rearrange("a (h d i) n -> h a d (i n)", h=2, d=HD)[half]
                        dst = k_stack[64 * half:64 * half + 3 * HD, g.mod(SBUFS)].bitcast(fp32)\
                            .rearrange("p s n -> p (s n)")
                        sp.dma_start(dst[0:HD], src[0]).then_inc(stack_loaded[par], 16)
                        sp.dma_start(dst[HD:3 * HD], src).then_inc(stack_loaded[par], 16)
                    if layer == 1:
                        at = a.count(1)
                        row = mask_dram[bass.ds(0 if at is None else at, 1), :].unsqueeze(1)\
                            .to_broadcast((1, SLOTS, T))
                        for p in (0, 64):
                            sp.dma_start(k_stack[p + ROW_MASK:p + ROW_MASK + 1, g.mod(SBUFS)].bitcast(fp32), row)\
                                .then_inc(mask_loaded[par], 16)

            for layer in range(LAYERS):
                for t in steps(sp, B, 5, 4):
                    step(layer, t)
                if layer == 0:
                    sp.wait_ge(m_y, 2 * NCH)
                    sp.dma_start(w1[:], w1_in[1]).then_inc(wm_loaded, 16)
                    sp.dma_start(w2[:], w2_in[1]).then_inc(wm_loaded, 16)
            with sp.Fori(0, NCH) as i:
                when(m_added, i * 2 + (2 * NCH + 2))
                sp.dma_start(out.rearrange("(c t p) d -> p c t d", p=P, t=CT)[:, bass.ds(i, 1)].squeeze(1),
                             x_sb[:, bass.ds(i * (CT * D), CT * D)].rearrange("p (t d) -> p t d", d=D))\
                    .then_inc(out_stored, 16)
            sp.wait_ge(out_stored, 16 * NCH)

        @block.tensor
        def _(pe):
            mm, transpose = nc.tensor.matmul, nc.tensor.transpose

            pe.wait_ge(vec_loaded, 16 * VEC_LOADS)
            pe.wait_ge(silu_ready, 1)
            for j in range(6 * NF):
                for f in range(NF):
                    mm(g_bank[0][:, j * B:(j + 1) * B], ada0[:, f, j * P:(j + 1) * P], silu[:, f, :],
                       start=(f == 0), stop=(f == NF - 1))
            for j in range(4 * NF):
                for f in range(NF):
                    mm(g_bank[1][:, j * B:(j + 1) * B], ada1[:, f, j * P:(j + 1) * P], cond[:, f, :],
                       start=(f == 0), stop=(f == NF - 1))
            pe.wait_ge(wa_loaded, 16 * 2 * LAYERS)
            c0 = COLS["bv"][0]
            for m in range(NF):
                for f in range(NF):
                    last = mm(o_bank[0][:, m:m + 1], wproj[:, 1, f, m * P:(m + 1) * P], cols[:, c0 + f:c0 + f + 1],
                              start=(f == 0), stop=(f == NF - 1))
            last.then_inc(mods_ready, 1)
            pe.wait_ge(setup_done, 1)
            pe.wait_ge(rows_set, 96)
            pe.wait_ge(vones_set, 1)

            USES = [("xT", 0, 1, xmT_ready, 1), ("negmaxT", 1, 3, negmaxT_copied, 1), ("q", 0, 1, q_lo, 1),
                    ("k", 1, 1, k_lo, 1), ("v", 0, 1, v_copied, 1), ("oT0", 1, 4, attn_ready, 2),
                    ("oT1", 0, 4, attn_ready, 2), ("attnT", 1, 4, attnT_copied, 1), ("proj", 0, 4, y_copied, 1),
                    ("yT", 1, 4, x_added, 1)]

            def take(layer, t, name):
                at = [u[0] for u in USES].index(name)
                which = USES[at][1]
                for back in range(1, 6 * len(USES)):
                    ago, pos = divmod(at - back, len(USES))
                    user, its, behind, emptied, each = USES[pos]
                    when = t - (behind - ago)
                    if its == which and when.within(B):
                        g = in_layer(layer, when)
                        pe.wait_ge(emptied, g.count(each, 1 if user == "oT0" else each))
                        return g_bank[which]
                return g_bank[which]

            def scores(layer, g, h):
                p, blk = head_place(h)
                q, k = q_stack[p:p + ROW_MAX, g.mod(SBUFS), blk], k_stack[p:p + ROW_MAX, g.mod(SBUFS), blk]
                if h == 0:
                    pe.wait_ge(stack_loaded[g.mod(2)], g.half().count(16 * STACK_LOADS, 16 * STACK_LOADS))
                    if layer == 1:
                        first = B // 2 * 32
                        pe.wait_ge(mask_loaded[g.mod(2)], g.half().count(32, 32 - first))
                wait(pe, max_done, g.count(H, h - 1))
                bank = s_bank[h % 2]
                if layer == 0:
                    mm(bank[:, 0:P], q[:, 0:P], k[:, 0:P], start=True, stop=False)
                    mm(bank[:, 0:P], ident16[:], tri16[:], start=False, stop=True)
                    mm(bank[:, P:3 * P], q[:, P:T], k, start=True, stop=False)
                    last = mm(bank[:, 2 * P:3 * P], ident16[:], tri16[:], start=False, stop=True)
                else:
                    for i in range(NT):
                        last = mm(bank[:, i * T:(i + 1) * T], q[:, i * P:(i + 1) * P], k, start=True, stop=True)
                last.then_inc(s_ready, 1)

            def scoresT(layer, g, h):
                p, blk = head_place(h)
                q, k = q_stack[p:p + ROWS, g.mod(SBUFS), blk], k_stack[p:p + ROWS, g.mod(SBUFS), blk]
                if h == 0:
                    pe.wait_ge(max_loaded[g.mod(2)], g.half().count(32, 32))
                wait(pe, exp_done, g.count(H, h - 1))
                bank = st_bank[h % 2]
                first = P if layer == 0 else 0
                mm(bank[:, 0:T], k[:, 0:P], q, start=True, stop=(layer == 1))
                if layer == 0:
                    mm(bank[:, 0:P], tri16[:], ident16[:], start=False, stop=True)
                last = mm(bank[:, T:2 * T - first], k[:, P:T], q[:, first:T], start=True, stop=(layer == 1))
                if layer == 0:
                    last = mm(bank[:, T:T + P], tri16[:], ident16[:], start=False, stop=True)
                last.then_inc(st_ready, 1)

            def attend(layer, g, r):
                pe.wait_ge(exp_done, g.count(H, GROUP * (r + 1)))
                if r == 0:
                    pe.wait_ge(v_copied, g.count(1, 1))
                wait(pe, o_copied, g.count(NG, r - 1))
                bank = o_bank[r % 2]
                first = P if layer == 0 else 0
                for kt in range(NT):
                    for j in range(GROUP):
                        h = GROUP * r + j
                        lo = first if kt else 0
                        last = mm(bank[32 * j:32 * j + 32, lo:T], v_sb[:, g.mod(SBUFS), kt, h, :],
                                  probs[:, h % 8, kt * T:kt * T + T - lo], start=(kt == 0), stop=(kt == NT - 1),
                                  tile_position=(0, 32 * j), skip_group_check=True)
                last.then_inc(pv_done, 1)

            def step(layer, t):
                a, b, c, d = t - 1, t - 2, t - 3, t - 4
                ga, gb, gc, gd = (in_layer(layer, s) for s in (a, b, c, d))
                for s in range(H):
                    if b.within(B):
                        scores(layer, gb, s)
                    if s < LAG and d.within(B):
                        scoresT(layer, gd, s + H - LAG)
                    if s >= LAG and c.within(B):
                        scoresT(layer, gc, s - LAG)
                    if s == 0 and a.within(B):
                        pe.wait_ge(xn_ready, ga.count(1, 1))
                        bank = take(layer, t, "xT")
                        for f in range(NF):
                            for i in range(NT):
                                last = transpose(bank[:, f * T + i * P:f * T + (i + 1) * P],
                                                 xn[:, ga.mod(2), i, f * P:(f + 1) * P], ident[:])
                        last.then_inc(xT_ready, 1)
                    if s == 1 and c.within(B):
                        pe.wait_ge(negmax_ready, gc.count(1, 1))
                        bank = take(layer, t, "negmaxT")
                        for i in range(NT):
                            src = negmax[:, gc.mod(2), i].bitcast(fp32).rearrange("p a b s -> p (a b s)")
                            last = transpose(bank[0:32, i * P:(i + 1) * P], src, ident[:])
                        last.then_inc(negmaxT_ready, 1)
                    if s == 2:
                        if d.within(B):
                            attend(layer, gd, 2)
                        if a.within(B):
                            pe.wait_ge(xmT_ready, ga.count(1, 1))
                            project(layer, take(layer, t, "q"), ga, 0).then_inc(q_ready, 1)
                    if s == 4 and a.within(B):
                        project(layer, take(layer, t, "k"), ga, D).then_inc(k_ready, 1)
                    if s == 6:
                        if d.within(B):
                            attend(layer, gd, 3)
                        if a.within(B):
                            bank = take(layer, t, "v")
                            for i in range(NT):
                                for f in range(NF):
                                    last = mm(bank[:, i * D:(i + 1) * D], xmT[:, ga.mod(2), f, i * P:(i + 1) * P],
                                              wqkv[:, layer, f, 2 * D:3 * D], start=(f == 0), stop=(f == NF - 1))
                            last.then_inc(v_ready, 1)
                    if s in (8, 9) and d.within(B):
                        i = s - 8
                        if i == 0:
                            pe.wait_ge(o_copied, gd.count(NG, NG))
                        bank = take(layer, t, f"oT{i}")
                        for r in range(NG):
                            last = transpose(bank[:, r * P:(r + 1) * P], o_sb[:, gd.mod(2), r, i * P:(i + 1) * P],
                                             ident[:])
                        last.then_inc(oT_ready, 1)
                    if s == 10 and c.within(B):
                        attend(layer, gc, 0)
                    if s == 11 and d.within(B):
                        pe.wait_ge(attn_ready, gd.count(2, 2))
                        bank = take(layer, t, "attnT")
                        for f in range(NF):
                            for i in range(NT):
                                last = transpose(bank[:, f * T + i * P:f * T + (i + 1) * P],
                                                 attn[:, gd.mod(2), i, f * P:(f + 1) * P], ident[:])
                        last.then_inc(attnT_ready, 1)
                    if s == 13 and d.within(B):
                        pe.wait_ge(attnT_copied, gd.count(1, 1))
                        bank = take(layer, t, "proj")
                        for m in range(NF):
                            for f in range(NF):
                                last = mm(bank[:, m * T:(m + 1) * T], wproj[:, layer, f, m * P:(m + 1) * P],
                                          attnT[:, f, :], start=(f == 0), stop=(f == NF - 1))
                        last.then_inc(proj_ready, 1)
                    if s == 14 and c.within(B):
                        attend(layer, gc, 1)
                    if s == 15 and d.within(B):
                        pe.wait_ge(y_copied, gd.count(1, 1))
                        bank = take(layer, t, "yT")
                        for i in range(NT):
                            for f in range(NF):
                                last = transpose(bank[:, i * D + f * P:i * D + (f + 1) * P],
                                                 y_sb[:, f, i * P:(i + 1) * P], ident[:])
                        last.then_inc(yT_ready, 1)

            def project(layer, bank, g, first):
                for m in range(NF):
                    for f in range(NF):
                        last = mm(bank[:, m * T:(m + 1) * T],
                                  wqkv[:, layer, f, first + m * P:first + (m + 1) * P],
                                  xmT[:, g.mod(2), f, :], start=(f == 0), stop=(f == NF - 1))
                return last

            def mlp_step(layer, t):
                a, b, c = t, t - 1, t - 2
                ga, gb, gc = (s - (-NCH * layer) for s in (a, b, c))

                if a.within(NCH):
                    pe.wait_ge(m_xn, ga.count(1, 1))
                    for f in range(NF):
                        wait(pe, m_xmT, ga.count(2, f - 1))
                        for i in range(CT):
                            last = transpose(s_bank[f][:, i * P:(i + 1) * P],
                                             xn_m[:, ga.mod(2), i, f * P:(f + 1) * P], ident[:])
                        last.then_inc(m_xT, 1)
                for m in range(NM):
                    if m == NM // 2 and c.within(NCH):
                        pe.wait_ge(m_ycopied, gc.count(2, 2))
                        for i in range(2):
                            wait(pe, m_added, gc.count(2))
                            for k in range(2):
                                for f in range(NF):
                                    last = transpose(g_bank[i][:, k * D + f * P:k * D + (f + 1) * P],
                                                     y_m[:, gc.mod(2), f, (2 * i + k) * P:(2 * i + k + 1) * P],
                                                     ident[:])
                            last.then_inc(m_yT, 1)
                    if b.within(NCH):
                        if m == 0:
                            pe.wait_ge(m_xmT, gb.count(2, 2))
                        wait(pe, m_gelu, gb.count(NM, m - 1))
                        for f in range(NF):
                            last = mm(st_bank[m % 2][:, :], w1[:, f, m * P:(m + 1) * P], xmT_m[:, gb.mod(2), f, :],
                                      start=(f == 0), stop=(f == NF - 1))
                        last.then_inc(m_h, 1)
                if b.within(NCH):
                    for o in range(NF):
                        wait(pe, m_ycopied, gb.count(2, o - 1))
                        for m in range(NM):
                            if o == 0:
                                pe.wait_ge(m_gelu, gb.count(NM, m + 1))
                            last = mm(o_bank[o][:, :], w2[:, m, o * P:(o + 1) * P], hT[:, m, :],
                                      start=(m == 0), stop=(m == NM - 1))
                        last.then_inc(m_y, 1)

            for layer in range(LAYERS):
                for t in steps(pe, B, 5, 4):
                    step(layer, t)
                pe.wait_ge(x_added, B * (layer + 1))
                pe.wait_ge(wm_loaded, 32 * (layer + 1))
                for t in steps(pe, NCH, 3, 2):
                    mlp_step(layer, t)
                pe.wait_ge(m_added, 2 * NCH * (layer + 1))

        @block.scalar
        def _(act):
            activation = nc.scalar.activation
            act.wait_ge(vec_loaded, 16 * VEC_LOADS)
            activation(sig[:], cond[:], ACT.Exp, scale=-1.0).then_inc(expneg, 1)
            act.wait_ge(setup_done, 1)
            act.wait_ge(rows_set, 96)
            cq = COLS["bqk"][0]

            def step(layer, t):
                a, c, d = t - 1, t - 3, t - 4
                ga, gc, gd = (in_layer(layer, s) for s in (a, c, d))

                def exponentials(g, h):
                    act.wait_ge(st_ready, g.count(H, h + 1))
                    wait(act, pv_done, g.count(NG, h // GROUP - 1))
                    n = 3 * P if layer == 0 else 4 * P
                    activation(probs[:, h % 8, 0:n], st_bank[h % 2][:, 0:n], ACT.Exp, scale=SCALE)\
                        .then_inc(exp_done, 1)

                def outputs(g, r):
                    act.wait_ge(pv_done, g.count(NG, r + 1))
                    if r == 0:
                        wait(act, oT_ready, g.count(2, -2))
                    activation(o_sb[:, g.mod(2), r, :], o_bank[r % 2][:, 0:T], ACT.Copy).then_inc(o_copied, 1)

                def high(ready, done, stored, bank, split, first):
                    act.wait_ge(ready, ga.count(1, 1))
                    wait(act, stored, ga.count(16))
                    if layer == 0:
                        activation(split[:, 0], bank[:].rearrange("p (f n) -> p f n", f=NF), ACT.Copy)\
                            .then_inc(done, 1)
                    else:
                        for f in range(NF):
                            last = activation(split[:, 0, f], bank[:, f * T:(f + 1) * T], ACT.Identity,
                                              bias=cols[:, cq + first + f:cq + first + f + 1])
                        last.then_inc(done, 1)

                for s in range(H):
                    if s < LAG and d.within(B):
                        exponentials(gd, s + H - LAG)
                    if s >= LAG and c.within(B):
                        exponentials(gc, s - LAG)
                    if s == 0 and a.within(B):
                        act.wait_ge(xT_ready, ga.count(1, 1))
                        wait(act, v_ready, ga.count(1, -1))
                        for f in range(NF):
                            last = activation(xmT[:, ga.mod(2), f], g_bank[0][:, f * T:(f + 1) * T], ACT.Identity,
                                              scale=tab(layer, A1, f, a), bias=tab(layer, B1, f, a))
                        last.then_inc(xmT_ready, 1)
                    if s == 1 and c.within(B):
                        act.wait_ge(negmaxT_ready, gc.count(1, 1))
                        wait(act, max_loaded[gc.mod(2)], gc.half().count(32))
                        activation(negmaxT[:, gc.mod(2), :], g_bank[1][0:32, 0:T], ACT.Copy)\
                            .then_inc(negmaxT_copied, 1)
                    if s == 2:
                        if d.within(B):
                            outputs(gd, 2)
                        if a.within(B):
                            high(q_ready, q_hi, q_stored, g_bank[0], q_split, 0)
                    if s == 4 and a.within(B):
                        high(k_ready, k_hi, k_stored, g_bank[1], k_split, NF)
                    if s == 6:
                        if d.within(B):
                            outputs(gd, 3)
                        if a.within(B):
                            act.wait_ge(v_ready, ga.count(1, 1))
                            wait(act, pv_done, ga.count(NG, NG - SBUFS * NG))
                            activation(v_sb[:, ga.mod(SBUFS), :, :, 0:HD],
                                       g_bank[0][:].rearrange("p (i h d) -> p i h d", i=NT, h=H), ACT.Copy)\
                                .then_inc(v_copied, 1)
                    if s == 10 and c.within(B):
                        outputs(gc, 0)
                    if s == 11 and d.within(B):
                        act.wait_ge(attnT_ready, gd.count(1, 1))
                        wait(act, proj_ready, gd.count(1))
                        activation(attnT[:], g_bank[1][:].rearrange("p (f n) -> p f n", f=NF), ACT.Copy)\
                            .then_inc(attnT_copied, 1)
                    if s == 13 and d.within(B):
                        act.wait_ge(proj_ready, gd.count(1, 1))
                        wait(act, yT_ready, gd.count(1))
                        for f in range(NF):
                            last = activation(y_sb[:, f], g_bank[0][:, f * T:(f + 1) * T], ACT.Identity,
                                              scale=tab(layer, G1, f, d), bias=tab(layer, GB1, f, d))
                        last.then_inc(y_copied, 1)
                    if s == 14 and c.within(B):
                        outputs(gc, 1)

            def mlp_step(layer, t):
                a, b = t, t - 1
                ga, gb = (s - (-NCH * layer) for s in (a, b))

                def modulate(dst, src, f, scale, shift, chunk):
                    for k in range(2):
                        batch = Step(chunk.const * 2 + k, chunk.reg, chunk.stride * 2)
                        last = activation(dst[:, k * T:(k + 1) * T], src[:, k * T:(k + 1) * T], ACT.Identity,
                                          scale=tab(layer, scale, f, batch), bias=tab(layer, shift, f, batch))
                    return last

                if a.within(NCH):
                    for f in range(NF):
                        act.wait_ge(m_xT, ga.count(2, f + 1))
                        if f == 0:
                            wait(act, m_h, ga.count(NM, -NM))
                        modulate(xmT_m[:, ga.mod(2), f], s_bank[f], f, A2, B2, a).then_inc(m_xmT, 1)
                if b.within(NCH):
                    cb = COLS[f"b1_{layer}"][0]
                    wait(act, m_y, gb.count(2))
                    for m in range(NM):
                        act.wait_ge(m_h, gb.count(NM, m + 1))
                        activation(hT[:, m, :], st_bank[m % 2][:, :], ACT.Gelu, bias=cols[:, cb + m:cb + m + 1])\
                            .then_inc(m_gelu, 1)
                    for f in range(NF):
                        act.wait_ge(m_y, gb.count(2, f + 1))
                        if f == 0:
                            wait(act, m_yT, gb.count(2, -2))
                        modulate(y_m[:, gb.mod(2), f], o_bank[f], f, G2, GB2, b).then_inc(m_ycopied, 1)

            for layer in range(LAYERS):
                if layer:
                    act.wait_ge(m_yT, 2 * NCH * layer)
                    act.wait_ge(vones_set, layer + 1)
                for t in steps(act, B, 5, 4):
                    step(layer, t)
                act.wait_ge(x_added, B * (layer + 1))
                for t in steps(act, NCH, 3, 2):
                    mlp_step(layer, t)

        @block.vector
        def _(dve):
            v = nc.vector
            links = [0]

            def link(ins):
                links[0] += 1
                ins.then_inc(chain, 1)
                dve.wait_ge(chain, links[0])

            v.memset(q_split[:].bitcast(fp32), 1.0).then_inc(ones_set, 1)
            v.memset(k_split[:].bitcast(fp32), 0.0).then_inc(ones_set, 1)
            dve.wait_ge(vec_loaded, 16 * VEC_LOADS)
            v.tensor_copy(ident16[:], ident[:])
            v.tensor_copy(tri16[:], tri[:])
            v.tensor_scalar(maskf[:], mask_int[:], BIG, None, ALU.mult).then_inc(maskf_ready, 1)
            dve.wait_ge(expneg, 1)
            link(v.tensor_scalar(sig[:], sig[:], 1.0, None, ALU.add))
            link(v.reciprocal(sig[:], sig[:]))
            v.tensor_tensor(silu[:], sig[:], cond[:], ALU.mult).then_inc(silu_ready, 1)
            dve.wait_ge(mods_ready, 1)

            def col(name, n):
                first, have = COLS[name]
                assert have == n
                return cols[:, first:first + n].unsqueeze(2).to_broadcast((P, n, B))

            def kind(layer, k):
                return table[layer][:, k * NF * B:(k + 1) * NF * B].rearrange("p (f b) -> p f b", f=NF)

            link(v.tensor_tensor(mod0[:], g_bank[0][:, 0:6 * NF * B].rearrange("p (j b) -> p j b", b=B),
                                 col("bada", 6 * NF), ALU.add))
            link(v.tensor_tensor(mod1[:], g_bank[1][:, 0:4 * NF * B].rearrange("p (j b) -> p j b", b=B),
                                 col("bada1", 4 * NF), ALU.add))
            c0 = COLS["bo"][0]
            link(v.tensor_tensor(bfold[:], o_bank[0][:, 0:NF], cols[:, c0:c0 + NF], ALU.add))
            for first, ka, kb, kg, kgb, g, be, bias in ((0, A1, B1, G1, GB1, "g1", "be1", "bproj"),
                                                        (3, A2, B2, G2, GB2, "g2", "be2", "b2_0")):
                shift, scale, gate = (mod0[:, (first + i) * NF:(first + i + 1) * NF, :] for i in range(3))
                v.scalar_tensor_tensor(out=kind(0, ka), in0=scale, scalar=1.0, in1=col(g, NF), op0=ALU.add,
                                       op1=ALU.mult)
                link(v.scalar_tensor_tensor(out=kind(0, kb), in0=scale, scalar=1.0, in1=col(be, NF), op0=ALU.add,
                                            op1=ALU.mult))
                v.tensor_tensor(kind(0, kb), kind(0, kb), shift, ALU.add)
                v.tensor_copy(kind(0, kg), gate)
                v.tensor_tensor(kind(0, kgb), gate, col(bias, NF), ALU.mult)
            for first, ka, kb, kg in ((0, A1, B1, G1), (2, A2, B2, G2)):
                v.tensor_scalar(kind(1, ka), mod1[:, first * NF:(first + 1) * NF, :], 1.0, None, ALU.add)
                v.tensor_copy(kind(1, kb), mod1[:, (first + 1) * NF:(first + 2) * NF, :])
                v.memset(kind(1, kg), 1.0)
            v.tensor_copy(kind(1, GB1), bfold[:].unsqueeze(2).to_broadcast((P, NF, B)))
            v.tensor_copy(kind(1, GB2), col("b2_1", NF)).then_inc(setup_done, 1)

            def statistics(rows, tiles, into, mean_var, part, done, g, used):
                wait(dve, used[0], used[1])
                for i in range(tiles):
                    v.bn_stats(into[:, i, :], rows[:, i * D:(i + 1) * D]).then_inc(part, 1)
                wait_apart(dve, part, g.count(tiles, tiles), dve_passed)
                for i in range(tiles):
                    last = v.bn_aggr(mean_var[:, i, :], into[:, i, :])
                last.then_inc(done, 1)

            def normalise(rows, tiles, dst, mean_var, rs, rdy, done, g):
                dve.wait_ge(rdy, g.count(1, 1))
                for i in range(tiles):
                    last = v.tensor_scalar(dst[:, i, :], rows[:, i * D:(i + 1) * D], mean_var[:, i, 0:1],
                                           rs[:, i:i + 1], ALU.subtract, ALU.mult)
                last.then_inc(done, 1)

            def low(layer, g, ready, done, bank, split, first):
                dve.wait_ge(ready, g.count(1, 1))
                c = COLS["bqk"][0] + first
                if layer == 0:
                    v.tensor_tensor(split[:, 1], bank[:].rearrange("p (f n) -> p f n", f=NF), split[:, 0],
                                    ALU.subtract).then_inc(done, 1)
                else:
                    for f in range(NF):
                        last = v.scalar_tensor_tensor(out=split[:, 1, f], in0=bank[:, f * T:(f + 1) * T],
                                                      scalar=cols[:, c + f:c + f + 1], in1=split[:, 0, f],
                                                      op0=ALU.add, op1=ALU.subtract)
                    last.then_inc(done, 1)

            def step(layer, t):
                n, a, b, d = t, t - 1, t - 2, t - 4
                gn, ga, gb, gd = (in_layer(layer, s) for s in (n, a, b, d))
                for s in range(H):
                    if b.within(B):
                        if s == 0:
                            wait(dve, negmax_ready, gb.count(1, -1))
                        dve.wait_ge(s_ready, gb.count(H, s + 1))
                        if layer == 0:
                            v.reduce_max(maxima[:, gb.mod(2), s, 0:3],
                                         s_bank[s % 2][:, 0:3 * P].rearrange("p (i n) -> p i n", n=P), AX.X)\
                                .then_inc(max_done, 1)
                        else:
                            v.reduce_max(maxima[:, gb.mod(2), s, 0:2],
                                         s_bank[s % 2][:].rearrange("p (i n) -> p i n", n=T), AX.X)\
                                .then_inc(max_done, 1)
                    if s == 2 and a.within(B):
                        low(layer, ga, q_hi, q_lo, g_bank[0], q_split, 0)
                    if s == 4 and a.within(B):
                        low(layer, ga, k_hi, k_lo, g_bank[1], k_split, NF)
                    if s == 10 and n.within(B):
                        if n.reg is None:
                            dve.wait_ge(x_loaded[n.const // 4], 16)
                        elif layer == 0 and n.const == 4:
                            for i in range(1, 4):
                                dve.wait_ge(x_loaded[i], 16)
                        statistics(xrows(n, NT), NT, stats[:, gn.mod(2)], mv[:, gn.mod(2)], stats_part, mv_ready, gn,
                                   (xn_ready, gn.count(1, -1)))
                    if s == 12 and n.within(B):
                        wait(dve, xT_ready, gn.count(1, -1))
                        normalise(xrows(n, NT), NT, xn[:, gn.mod(2)], mv[:, gn.mod(2)], rstd[:, gn.mod(2)],
                                  rstd_ready, xn_ready, gn)
                    if s in (8, 9) and d.within(B):
                        i = s - 8
                        dve.wait_ge(oT_ready, gd.count(2, i + 1))
                        if i == 0:
                            wait(dve, attnT_ready, gd.count(1))
                        o = g_bank[1 - i][:].rearrange("p (h n) -> p h n", n=32)
                        wait(dve, attn_ready, gd.count(2, i))
                        v.reciprocal(rsum[:, i], o[:, :, HD]).then_inc(rsum_ready, 1)
                        dve.wait_ge(rsum_ready, gd.count(2, i + 1))
                        v.tensor_tensor(attn[:, gd.mod(2), i].rearrange("p (h n) -> p h n", n=HD), o[:, :, 0:HD],
                                        rsum[:, i].unsqueeze(2).to_broadcast((P, H, HD)), ALU.mult)\
                            .then_inc(attn_ready, 1)
                if b.within(B):
                    m = maxima[:, gb.mod(2)]
                    dve.wait_ge(max_done, gb.count(H, H))
                    if layer == 0:
                        v.tensor_tensor(m[:, :, 1], m[:, :, 1], m[:, :, 2], ALU.max).then_inc(max_joined, 1)
                        dve.wait_ge(max_joined, gb.count(1, 1))
                    wait(dve, negmaxT_ready, gb.count(1, -1))
                    for i in range(NT):
                        src = m[:, :, i].rearrange("p (f j e) -> p e j f", f=2, e=2)
                        dst = negmax[:, gb.mod(2), i].rearrange("p e c (j f) -> p e c j f", f=2)
                        last = v.tensor_scalar(dst[:, :, 0], src, -1.0, None, ALU.mult)
                    last.then_inc(negmax_hi, 1)
                    dve.wait_ge(negmax_hi, gb.count(1, 1))
                    for i in range(NT):
                        src = m[:, :, i].rearrange("p (f j e) -> p e j f", f=2, e=2)
                        dst = negmax[:, gb.mod(2), i].rearrange("p e c (j f) -> p e c j f", f=2)
                        for e in range(2):
                            last = v.scalar_tensor_tensor(out=dst[:, e, 1], in0=src[:, e], scalar=-1.0,
                                                          in1=dst[:, e, 0], op0=ALU.mult, op1=ALU.subtract)
                    last.then_inc(negmax_ready, 1)
                if d.within(B):
                    dve.wait_ge(yT_ready, gd.count(1, 1))
                    rows = xrows(d, NT)
                    v.tensor_tensor(rows, g_bank[1][:], rows, ALU.add).then_inc(x_added, 1)

            def mlp_step(layer, t):
                a, c = t, t - 2
                ga, gc = (s - (-NCH * layer) for s in (a, c))
                if a.within(NCH):
                    b = Step(a.const * 2, a.reg, a.stride * 2)
                    rows = xrows(b, CT)
                    statistics(rows, CT, stats_m[:, ga.mod(2)], mv_m[:, ga.mod(2)], m_stats, m_mv, ga,
                               (m_xn, ga.count(1, -1)))
                    wait(dve, m_xT, ga.count(2, -2))
                    normalise(rows, CT, xn_m[:, ga.mod(2)], mv_m[:, ga.mod(2)], rstd_m[:, ga.mod(2)], m_rstd, m_xn,
                              ga)
                if c.within(NCH):
                    b = Step(c.const * 2, c.reg, c.stride * 2)
                    for i in range(2):
                        dve.wait_ge(m_yT, gc.count(2, i + 1))
                        rows = xrows(b, 2, 2 * i)
                        v.tensor_tensor(rows, g_bank[i][:], rows, ALU.add).then_inc(m_added, 1)

            for layer in range(LAYERS):
                if layer:
                    dve.wait_ge(m_added, 2 * NCH * layer)
                for t in steps(dve, B, 5, 4):
                    step(layer, t)
                dve.wait_ge(x_added, B * (layer + 1))
                dve.wait_ge(oT_ready, 2 * B * (layer + 1))
                for t in steps(dve, NCH, 3, 2):
                    mlp_step(layer, t)

        @block.gpsimd
        def _(pool):
            g_ = nc.gpsimd

            g_.memset(half_power[:], -0.5).then_inc(power_set, 1)
            pool.wait_ge(power_set, 1)

            def inverse_deviation(dst, var, tiles, shifted, g, done):
                g_.tensor_scalar(dst, var, EPS, 1.0, ALU.add, ALU.mult).then_inc(shifted, 1)
                pool.wait_ge(shifted, g.count(1, 1))
                g_.tensor_tensor(dst, dst, half_power[:, 0:tiles], ALU.pow).then_inc(done, 1)

            def step(layer, t):
                n, gn = t, in_layer(layer, t)
                if n.within(B):
                    wait_apart(pool, mv_ready, gn.count(1, 1), pool_passed)
                    inverse_deviation(rstd[:, gn.mod(2)], mv[:, gn.mod(2), :, 1], NT, var_shifted, gn, rstd_ready)

            def mlp_step(layer, t):
                if t.within(NCH):
                    g = t - (-NCH * layer)
                    wait_apart(pool, m_mv, g.count(1, 1), pool_passed)
                    inverse_deviation(rstd_m[:, g.mod(2)], mv_m[:, g.mod(2), :, 1], CT, m_shifted, g, m_rstd)

            for layer in range(LAYERS):
                if layer:
                    pool.wait_ge(m_yT, 2 * NCH * layer)
                g_.memset(v_sb[:, :, :, :, HD:32], 1.0).then_inc(vones_set, 1)
                for t in steps(pool, B, 5, 4):
                    step(layer, t)
                for t in steps(pool, NCH, 3, 2):
                    mlp_step(layer, t)


def kernel(**inputs):
    import numpy as np
    import concourse.bacc as bacc
    from concourse.bass_utils import run_bass_kernel_spmd

    a = {k: np.asarray(v) for k, v in inputs.items()}

    def rows(w):
        return np.ascontiguousarray(w.reshape(-1, P, w.shape[1]).transpose(1, 0, 2))

    def columns(v):
        return v.reshape(-1, P).T

    order = np.array([((4 * t + i) * 2 + par) * HD + d
                      for t in range(NF) for par in range(2) for d in range(HD) for i in range(4)])
    wqkv0 = a["L0_cond_Wqkv"]
    q0, k0, v0 = wqkv0[:, 0:D], wqkv0[:, D:2 * D], wqkv0[:, 2 * D:]
    q1, k1, v1 = a["L1_cond_wq"].T, a["L1_cond_wk"].T, a["L1_cond_wv"].T
    vectors = {"g1": a["L0_cond_g1"], "be1": a["L0_cond_be1"], "g2": a["L0_cond_g2"], "be2": a["L0_cond_be2"],
               "bproj": a["L0_cond_bproj"], "b2_0": a["L0_cond_b2"], "b1_0": a["L0_cond_b1"],
               "bada": a["L0_cond_bada"], "bada1": np.concatenate([a["L1_cond_b_adaln1"], a["L1_cond_b_adaln2"]]),
               "bqk": np.concatenate([a["L1_cond_bq"][order], a["L1_cond_bk"][order]]), "bv": a["L1_cond_bv"],
               "bo": a["L1_cond_bo"], "b1_1": a["L1_cond_b1"], "b2_1": a["L1_cond_b2"]}
    mask_words = np.zeros((B, T, 4), np.uint8)
    mask_words[:, :, 0] = a["mask_BxS_bf0"].view(np.uint8)
    arrays = {
        "x_in": a["x"].reshape(B * T, D),
        "cond_in": rows(a["cond_1024"].T),
        "mask_in": mask_words.view(np.int32)[:, :, 0],
        "wqkv_in": np.stack([rows(np.concatenate([q0[:, order], k0[:, order], v0], axis=1)),
                             rows(np.concatenate([q1[:, order], k1[:, order], v1], axis=1))]),
        "wproj_in": np.stack([rows(a["L0_cond_Wproj"]), rows(a["L1_cond_wo"].T)]),
        "w1_in": np.stack([rows(a["L0_cond_W1"]), rows(a["L1_cond_w1"].T)]),
        "w2_in": np.stack([rows(a["L0_cond_W2"]), rows(a["L1_cond_w2"].T)]),
        "ada0_in": rows(a["L0_cond_Wada"]),
        "ada1_in": rows(np.concatenate([a["L1_cond_w_adaln1"].T, a["L1_cond_w_adaln2"].T], axis=1)),
        "cols_in": np.concatenate([columns(vectors[name]) for name in COLS], axis=1),
        "ident_in": np.eye(P, dtype=np.float32),
        "tri_in": np.where(np.arange(P)[None, :] > np.arange(P)[:, None], BIG, 0.0).astype(np.float32),
    }
    nc = bacc.Bacc("TRN2", target_bir_lowering=False, num_devices=1)
    args = []
    for name in arrays:
        arrays[name] = np.ascontiguousarray(arrays[name])
        args.append(nc.dram_tensor(name, arrays[name].shape, mybir.dt.from_np(arrays[name].dtype),
                                   kind="ExternalInput").ap())
    out = nc.dram_tensor("out", (B * T, D), mybir.dt.float32, kind="ExternalOutput").ap()
    build(nc, *args, out)
    r = run_bass_kernel_spmd(nc, [arrays], core_ids=[0])
    return r.results[0]["out"].reshape(B, T, D)
```

```python
import concourse.bass as bass
from concourse import mybir
from contextlib import ExitStack

LAYERS, B, T, D = 2, 16, 256, 256
H, HD = 16, 16
F = 4 * D
P = 128
NF, NM, NT = D // P, F // P, T // P
EPS = 1e-5
SCALE = HD ** -0.5
BIG = -1e30
GROUP = 4
NG = H // GROUP
SLOTS = H // 2
SBUFS = 4
LAG = 5
S_BANK = [h % 3 for h in range(H - 1)] + [1]
S_AGO = [next(k for k in range(1, H) if S_BANK[h - k] == S_BANK[h]) for h in range(H)]
SLOT = {"q": (0, 1), "negmaxT": 1, "k": (3, 4), "v": (5, 7), "oT": (8, 9), "attnT": 11, "xT": 12, "proj": (13, 15)}
PV_SLOT = [(LAG + 5 + GROUP * i) % H for i in range(NG)]
ROW_MASK, ROW_MAX, ROWS = 3 * HD, 3 * HD + 1, 3 * HD + 3

COLS, _at = {}, 0
for _name, _n in [("g1", NF), ("be1", NF), ("g2", NF), ("be2", NF), ("b1_0", NM),
                  ("bada", 6 * NF), ("bada1", 4 * NF), ("bqk", 2 * NF), ("bv", NF), ("b1_1", NM)]:
    COLS[_name] = (_at, _n)
    _at += _n
NCOLS = _at
A1, B1, A2, B2 = KINDS = range(4)
COLUMN_PARTS, GATE_PARTS = (0, 1, 3, 4), (2, 5)
ROWS_IN = ["bproj", "b2_0", "bo", "b2_1", "gate_attn", "gate_mlp"]


class Step:

    def __init__(self, const, reg=None, stride=0):
        self.const, self.reg, self.stride = const, reg, stride

    def __sub__(self, k):
        return Step(self.const - k, self.reg, self.stride)

    def within(self, n):
        return self.reg is not None or 0 <= self.const < n

    def mod(self, m):
        return self.const % m

    def half(self):
        return Step(self.const // 2, self.reg, self.stride // 2)

    def count(self, each, plus=0):
        v = self.const * each + plus
        if self.reg is not None:
            return self.reg * (self.stride * each) + v
        return v if v > 0 else None


def wait(eng, sem, value):
    if value is not None:
        eng.wait_ge(sem, value)


def wait_apart(eng, sem, value, passed):
    if value is not None:
        eng.wait_ge(sem, value)
        eng.sem_inc(passed, 1)


def steps(eng, n, first, stages, unroll):
    last = n + stages - 1
    turns = (n - first) // unroll
    for t in range(first):
        yield Step(t)
    with eng.Fori(0, turns) as i:
        for u in range(unroll):
            yield Step(first + u, i, unroll)
    for t in range(first + turns * unroll, last):
        yield Step(t)


def head_place(h):
    pair, parity = h // 2, h % 2
    tile, i = pair // 4, pair % 4
    return 64 * parity, i * NF + tile


def build(nc, x_in, cond_in, mask_in, wa_in, w1_in, w2_in, ada0_in, ada1_in, cols_in, rows_in, ident_in,
          tri_in, out):
    fp32, f32r, bf16 = mybir.dt.float32, mybir.dt.float32r, mybir.dt.bfloat16
    ALU, ACT, AX = mybir.AluOpType, mybir.ActivationFunctionType, mybir.AxisListType

    with ExitStack() as ctx:
        def sb(name, shape, dt=fp32):
            return ctx.enter_context(nc.sbuf_tensor(name, shape, dt))

        def bank(name):
            return ctx.enter_context(nc.psum_tensor(name, [P, 512], fp32))

        def sem(name):
            return ctx.enter_context(nc.semaphore(name))

        x_sb = sb("x_sb", [P, B * NT * D])
        wa = sb("wa", [P, 2, NF, 4 * D], f32r)
        wm_raw = sb("wm_raw", [P, NF * F + NM * D])
        cols = sb("cols", [P, NCOLS])
        ident = sb("ident", [P, P])
        ident16 = sb("ident16", [P, P], bf16)
        tri16 = sb("tri16", [P, P], bf16)
        table = [sb(f"table{l}", [P, len(KINDS) * NF * B]) for l in range(LAYERS)]
        q_stack = sb("q_stack", [P, SBUFS, SLOTS, T], f32r)
        k_stack = sb("k_stack", [P, SBUFS, SLOTS, T], f32r)
        v_sb = sb("v_sb", [P, SBUFS, NT, H, 32])
        probs = sb("probs", [P, 8, 512])
        stats = sb("stats", [P, 2, NT, 6])
        mv = sb("mv", [P, 2, NT, 2])
        rstd = sb("rstd", [P, 2, NT])
        xn = sb("xn", [P, 2, NT, D])
        xm_full = sb("xm_full", [P, NF, T])
        xmT = sb("xmT", [P, 2, 2, NF, T], f32r)
        qk_split = sb("qk_split", [P, 2, 2, NF, T], f32r)
        q_split, k_split = qk_split[:, 0], qk_split[:, 1]
        maxima = sb("maxima", [P, 2, H, 3])
        negmax = sb("negmax", [P, 2, NT, 2, 2, SLOTS], f32r)
        negmaxT = sb("negmaxT", [32, T], f32r)
        o_sb = sb("o_sb", [P, 2, NG, T])
        rsum = sb("rsum", [P, 2, H])
        attn = sb("attn", [P, NT, D])
        attnT = sb("attnT", [P, 2, NF, T], f32r)
        y_sb = sb("y_sb", [P, NT, D])
        bias_rows = sb("bias_rows", [P, 2, D])
        gate_rows = sb("gate_rows", [P, 2, D])

        CH = 2 * T
        CT = CH // P
        v_flat = v_sb[:].rearrange("p a t h n -> p (a t h n)")
        o_flat = o_sb[:].rearrange("p a g n -> p (a g n)")
        maskf = negmaxT[0:B]
        xn_flat = xn[:].rearrange("p a t n -> p (a t n)")
        free = SBUFS // 2 * NT * H * 32

        def in_v(n):
            nonlocal free
            free += n
            return v_flat[:, free - n:free]

        cond, silu, sig, mod0, mod1 = (in_v(n * B).rearrange("p (j b) -> p j b", b=B)
                                       for n in (NF, NF, NF, len(COLUMN_PARTS) * NF, 4 * NF))
        tri = in_v(P)
        mask_int = in_v(T)[0:B].bitcast(mybir.dt.int32)
        bv_wide = in_v(NF * P).rearrange("p (f n) -> p f n", f=NF)
        gates = attn[0:B].rearrange("p i n -> p (i n)")
        ones_zeros = attnT[:].rearrange("p a f n -> p (a f n)")
        ones, zeros = ones_zeros[0:16], ones_zeros[32:40]
        ada0 = wm_raw[:, 0:NF * 6 * D].rearrange("p (f n) -> p f n", f=NF)
        ada1 = probs[:].rearrange("p a n -> p (a n)")[:, 0:NF * 4 * D].rearrange("p (f n) -> p f n", f=NF)
        wa_raw = [w[:, 0:NF * 4 * D].rearrange("p (f n) -> p f n", f=NF) for w in (o_flat, v_flat)]
        wo_raw = y_sb[:]
        w1_raw = wm_raw[:, 0:NF * F].rearrange("p (f n) -> p f n", f=NF)
        w2_raw = wm_raw[:, NF * F:].rearrange("p (m n) -> p m n", m=NM)
        q_flat = q_stack[:].rearrange("p a s n -> p (a s n)")
        w1 = q_flat[:, 0:2 * NF * F].rearrange("p (a f n) -> p a f n", a=2, f=NF)
        w2 = q_flat[:, 2 * NF * F:].rearrange("p (a m n) -> p a m n", a=2, m=NM)
        hT = k_stack[:].rearrange("p a s n -> p (a s n)").rearrange("p (a m n) -> p a m n", a=2, m=NM)
        h_full = probs[:, 0:2]
        xm_full_m = probs[:, 2:4]
        y_m = probs[:, 4:6].rearrange("p b (i n) -> p b i n", i=NT)
        xn_m = xn_flat.rearrange("p (t n) -> p t n", t=CT)
        xmT_m = qk_split[:].rearrange("p c a f n -> p (c a f n)").rearrange("p (a f n) -> p a f n", a=2, f=NF)
        stats_m = sb("stats_m", [P, CT, 6])
        mv_m = sb("mv_m", [P, CT, 2])
        rstd_m = sb("rstd_m", [P, CT])
        half_power = sb("half_power", [P, CT])

        q_dram = nc.dram_tensor("q_dram", (2, 2, P, NF * T), fp32, kind="Internal").ap()
        k_dram = nc.dram_tensor("k_dram", (2, 2, P, NF * T), fp32, kind="Internal").ap()
        gate_dram = nc.dram_tensor("gate_dram", (B, 2 * D), fp32, kind="Internal").ap()
        mask_dram = nc.dram_tensor("mask_dram", (B, T), fp32, kind="Internal").ap()

        s_bank = [bank(f"s_bank{i}") for i in range(3)]
        st_bank = [bank(f"st_bank{i}") for i in range(2)]
        o_bank = bank("o_bank")
        g_bank = [bank(f"g_bank{i}") for i in range(2)]

        vec_loaded = sem("vec_loaded")
        late_loaded = sem("late_loaded")
        x_loaded = [sem(f"x_loaded{i}") for i in range(4)]
        wa_loaded = sem("wa_loaded")
        wa_high, wa_split = sem("wa_high"), sem("wa_split")
        wm_loaded = sem("wm_loaded")
        w1_high, w1_split = sem("w1_high"), sem("w1_split")
        w2_high, w2_split = sem("w2_high"), sem("w2_split")
        bias_loaded = sem("bias_loaded")
        gate_loaded = [sem(f"gate_loaded{i}") for i in range(2)]
        ones_set = sem("ones_set")
        rows_set = sem("rows_set")
        vones_set = sem("vones_set")
        chain = sem("chain")
        expneg = sem("expneg")
        silu_ready = sem("silu_ready")
        mods_ready = sem("mods_ready")
        bv_spread = sem("bv_spread")
        setup_done = sem("setup_done")
        gates_ready = sem("gates_ready")
        gates_stored = sem("gates_stored")
        maskf_ready = sem("maskf_ready")
        mask_stored = sem("mask_stored")
        stats_part = sem("stats_part")
        power_set = sem("power_set")
        sp_passed, dve_passed, pool_passed = sem("sp_passed"), sem("dve_passed"), sem("pool_passed")
        var_shifted = sem("var_shifted")
        m_shifted = sem("m_shifted")
        mv_ready = sem("mv_ready")
        rstd_ready = sem("rstd_ready")
        xn_ready = sem("xn_ready")
        xT_ready = sem("xT_ready")
        xm_high = sem("xm_high")
        xmT_ready = sem("xmT_ready")
        q_ready = sem("q_ready")
        k_ready = sem("k_ready")
        v_ready = sem("v_ready")
        q_hi = sem("q_hi")
        k_hi = sem("k_hi")
        q_lo = sem("q_lo")
        k_lo = sem("k_lo")
        v_copied = sem("v_copied")
        q_stored = sem("q_stored")
        k_stored = sem("k_stored")
        stack_loaded = [sem(f"stack_loaded{i}") for i in range(2)]
        mask_loaded = [sem(f"mask_loaded{i}") for i in range(2)]
        max_loaded = [sem(f"max_loaded{i}") for i in range(2)]
        s_ready = sem("s_ready")
        max_done = sem("max_done")
        max_joined = sem("max_joined")
        negmax_hi = sem("negmax_hi")
        negmax_ready = sem("negmax_ready")
        negmaxT_ready = sem("negmaxT_ready")
        negmaxT_copied = sem("negmaxT_copied")
        st_ready = sem("st_ready")
        exp_done = sem("exp_done")
        pv_done = sem("pv_done")
        o_copied = sem("o_copied")
        oT_ready = sem("oT_ready")
        rsum_ready = sem("rsum_ready")
        attn_ready = sem("attn_ready")
        attnT_ready = sem("attnT_ready")
        attnT_hi = sem("attnT_hi")
        attnT_lo = sem("attnT_lo")
        proj_ready = sem("proj_ready")
        y_copied = sem("y_copied")
        y_gated = sem("y_gated")
        x_added = sem("x_added")
        m_stats = sem("m_stats")
        m_mv = sem("m_mv")
        m_rstd = sem("m_rstd")
        m_xn = sem("m_xn")
        m_xT = sem("m_xT")
        m_xhigh = sem("m_xhigh")
        m_xmT = sem("m_xmT")
        m_h = sem("m_h")
        m_gelu = sem("m_gelu")
        m_hhigh = sem("m_hhigh")
        m_hT = sem("m_hT")
        m_y = sem("m_y")
        m_ycopied = sem("m_ycopied")
        m_added = sem("m_added")
        out_stored = sem("out_stored")

        block = ctx.enter_context(nc.Block())
        NCH = B * T // CH
        GATE_AT = ROWS_IN.index("gate_attn") * D
        VEC_LOADS, LATE_LOADS, STACK_LOADS = 5, 6, 8

        def tab(layer, kind, f, b):
            at = b.count(1, (kind * NF + f) * B)
            return table[layer][:, bass.ds(0 if at is None else at, 1)]

        def xrows(b, tiles, first=0):
            at = b.count(NT * D, first * D)
            return x_sb[:, bass.ds(0 if at is None else at, tiles * D)]

        def in_layer(layer, b):
            return b - (-B * layer)

        @block.sync
        def _(sp):
            def row(name):
                at = ROWS_IN.index(name)
                return rows_in[at:at + 1, :]

            for dst, src in [(cond, cond_in), (cols[:], cols_in), (ident[:], ident_in), (ada0, ada0_in)]:
                sp.dma_start(dst, src).then_inc(vec_loaded, 16)
            sp.dma_start(gates, rows_in.rearrange("r n -> (r n)")[GATE_AT:].unsqueeze(0).to_broadcast((B, 2 * D)))\
                .then_inc(vec_loaded, 16)
            n = B * NT // 4
            xt = x_in.rearrange("(t p) d -> p t d", p=P)

            def load_x(i):
                sp.dma_start(x_sb[:, i * n * D:(i + 1) * n * D].rearrange("p (t d) -> p t d", d=D),
                             xt[:, i * n:(i + 1) * n, :]).then_inc(x_loaded[i], 16)

            load_x(0)
            sp.dma_start(wa_raw[0], wa_in[0]).then_inc(wa_loaded, 16)
            for dst, src in [(mask_int, mask_in), (tri, tri_in), (ada1, ada1_in), (wo_raw, wa_in[1][:, :, 3 * D:]),
                             (bias_rows[:, 0], row("bproj").to_broadcast((P, D))),
                             (bias_rows[:, 1], row("bo").to_broadcast((P, D)))]:
                sp.dma_start(dst, src).then_inc(late_loaded, 16)
            for i in range(1, 4):
                load_x(i)

            def constant_rows(layer):
                sp.wait_ge(ones_set, 2 * (layer + 1))
                for p in (0, 64):
                    qs, ks = (x[:].rearrange("p a s n -> p (a s n)").bitcast(fp32) for x in (q_stack, k_stack))
                    sp.dma_start(qs[p + ROW_MASK:p + ROW_MASK + 1, :], ones[0:8].bitcast(fp32)).then_inc(rows_set, 16)
                    sp.dma_start(ks[p + ROW_MAX:p + ROW_MAX + 2, :], ones.bitcast(fp32)).then_inc(rows_set, 16)
                    if layer == 0:
                        sp.dma_start(ks[p + ROW_MASK:p + ROW_MASK + 1, :], zeros.bitcast(fp32)).then_inc(rows_set, 16)

            constant_rows(0)
            sp.wait_ge(gates_ready, 1)
            sp.dma_start(gate_dram, gates).then_inc(gates_stored, 16)
            sp.wait_ge(mods_ready, 1)
            sp.dma_start(w1_raw, w1_in[0]).then_inc(wm_loaded, 16)
            sp.dma_start(w2_raw, w2_in[0]).then_inc(wm_loaded, 16)
            sp.wait_ge(maskf_ready, 1)
            sp.dma_start(mask_dram, maskf.bitcast(fp32)).then_inc(mask_stored, 16)
            sp.wait_ge(mask_stored, 16)
            sp.wait_ge(gates_stored, 16)

            def load_gates(b, kind):
                at = b.count(1)
                sp.dma_start(gate_rows[:, b.mod(2)], gate_dram[bass.ds(0 if at is None else at, 1),
                                                               kind * D:(kind + 1) * D].to_broadcast((P, D)))\
                    .then_inc(gate_loaded[b.mod(2)], 16)

            def when(sem, value):
                wait_apart(sp, sem, value, sp_passed)

            def step(layer, t):
                c, a = t - 3, t - 1
                if c.within(B):
                    g = in_layer(layer, c)
                    when(negmaxT_copied, g.count(1, 1))
                    for p, first in ((0, 0), (64, 16)):
                        sp.dma_start(q_stack[p + ROW_MAX:p + ROW_MAX + 2, g.mod(SBUFS)].bitcast(fp32),
                                     negmaxT[first:first + 16].bitcast(fp32))\
                            .then_inc(max_loaded[g.mod(2)], 16)
                    if layer == 0:
                        when(x_added, c.count(1, -1))
                        load_gates(c, 0)
                if a.within(B):
                    g = in_layer(layer, a)
                    par = g.mod(2)
                    when(stack_loaded[par], g.half().count(16 * STACK_LOADS))
                    when(q_lo, g.count(1, 1))
                    sp.dma_start(q_dram[par].rearrange("a p n -> p a n"),
                                 q_split[:].bitcast(fp32).rearrange("p a f n -> p a (f n)")).then_inc(q_stored, 16)
                    when(k_lo, g.count(1, 1))
                    sp.dma_start(k_dram[par].rearrange("a p n -> p a n"),
                                 k_split[:].bitcast(fp32).rearrange("p a f n -> p a (f n)")).then_inc(k_stored, 16)
                    when(st_ready, g.count(H, H - SBUFS * H))
                    when(q_stored, g.count(16, 16))
                    for half in (0, 1):
                        src = q_dram[par].rearrange("a (h d i) n -> h a d (i n)", h=2, d=HD)[half]
                        dst = q_stack[64 * half:64 * half + 3 * HD, g.mod(SBUFS)].bitcast(fp32)\
                            .rearrange("p s n -> p (s n)")
                        sp.dma_start(dst[0:2 * HD], src).then_inc(stack_loaded[par], 16)
                        sp.dma_start(dst[2 * HD:3 * HD], src[0]).then_inc(stack_loaded[par], 16)
                    when(k_stored, g.count(16, 16))
                    for half in (0, 1):
                        src = k_dram[par].rearrange("a (h d i) n -> h a d (i n)", h=2, d=HD)[half]
                        dst = k_stack[64 * half:64 * half + 3 * HD, g.mod(SBUFS)].bitcast(fp32)\
                            .rearrange("p s n -> p (s n)")
                        sp.dma_start(dst[0:HD], src[0]).then_inc(stack_loaded[par], 16)
                        sp.dma_start(dst[HD:3 * HD], src).then_inc(stack_loaded[par], 16)
                    if layer == 1:
                        at = a.count(1)
                        row = mask_dram[bass.ds(0 if at is None else at, 1), :].unsqueeze(1)\
                            .to_broadcast((1, SLOTS, T))
                        for p in (0, 64):
                            sp.dma_start(k_stack[p + ROW_MASK:p + ROW_MASK + 1, g.mod(SBUFS)].bitcast(fp32), row)\
                                .then_inc(mask_loaded[par], 16)

            def mlp_gates(eng):
                yield Step(0)
                yield Step(1)
                with eng.Fori(0, NCH - 2) as i:
                    yield Step(2, i, 1)

            for layer in range(LAYERS):
                for t in steps(sp, B, 4, 5, 4):
                    step(layer, t)
                if layer == 0:
                    sp.wait_ge(y_copied, B)
                    sp.dma_start(bias_rows[:, 0], row("b2_0").to_broadcast((P, D))).then_inc(bias_loaded, 16)
                    sp.wait_ge(o_copied, NG * B)
                    sp.dma_start(wa_raw[1], wa_in[1]).then_inc(wa_loaded, 16)
                    for c in mlp_gates(sp):
                        for i in range(2):
                            b = Step(c.const * 2 + i, c.reg, c.stride * 2)
                            if c.reg is None and c.const == 0:
                                sp.wait_ge(x_added, B - 1 + i)
                            else:
                                when(m_added, b.count(1, -1))
                            load_gates(b, 1)
                        if c.reg is None and c.const == 1:
                            sp.wait_ge(w1_split, NM)
                            sp.wait_ge(w2_split, NM)
                            sp.dma_start(w1_raw, w1_in[1]).then_inc(wm_loaded, 16)
                            sp.dma_start(w2_raw, w2_in[1]).then_inc(wm_loaded, 16)
                    sp.wait_ge(m_ycopied, 2 * NCH)
                    constant_rows(1)
                    sp.dma_start(bias_rows[:, 0], row("b2_1").to_broadcast((P, D))).then_inc(bias_loaded, 16)
            with sp.Fori(0, NCH) as i:
                when(m_added, i * 2 + (2 * NCH + 2))
                sp.dma_start(out.rearrange("(c t p) d -> p c t d", p=P, t=CT)[:, bass.ds(i, 1)].squeeze(1),
                             x_sb[:, bass.ds(i * (CT * D), CT * D)].rearrange("p (t d) -> p t d", d=D))\
                    .then_inc(out_stored, 16)
            sp.wait_ge(out_stored, 16 * NCH)

        @block.tensor
        def _(pe):
            mm, transpose = nc.tensor.matmul, nc.tensor.transpose

            pe.wait_ge(vec_loaded, 16 * VEC_LOADS)
            pe.wait_ge(silu_ready, 1)
            for n, part in enumerate(COLUMN_PARTS):
                for m in range(NF):
                    at, j = part * D + m * P, n * NF + m
                    for f in range(NF):
                        mm(g_bank[0][:, j * B:(j + 1) * B], ada0[:, f, at:at + P], silu[:, f],
                           start=(f == 0), stop=(f == NF - 1))
            for n, part in enumerate(GATE_PARTS):
                for f in range(NF):
                    last = mm(g_bank[1][0:B, n * D:(n + 1) * D], silu[:, f], ada0[:, f, part * D:(part + 1) * D],
                              start=(f == 0), stop=(f == NF - 1))
            last.then_inc(mods_ready, 1)

            def set_up_layer1():
                pe.wait_ge(late_loaded, 16 * LATE_LOADS)
                for j in range(4 * NF):
                    for f in range(NF):
                        mm(s_bank[0][:, j * B:(j + 1) * B], ada1[:, f, j * P:(j + 1) * P], cond[:, f],
                           start=(f == 0), stop=(f == NF - 1))
                pe.wait_ge(bv_spread, 1)
                for f in range(NF):
                    last = mm(s_bank[1][:, 0:D], bv_wide[:, f], wo_raw[:, f], start=(f == 0), stop=(f == NF - 1))
                last.then_inc(mods_ready, 1)
                pe.wait_ge(setup_done, 2)

            TERMS = [(0, 0), (1, 0), (0, 1)]

            def product(dst, weights, rows, f, tiles):
                for n, (i, j) in enumerate(TERMS):
                    last = mm(dst, weights[i], rows[j], start=(f == 0 and n == 0),
                              stop=(f == tiles - 1 and n == len(TERMS) - 1))
                return last

            USES = [("q", 1, 1, q_lo, 1), ("negmaxT", 0, 3, negmaxT_copied, 1), ("k", 0, 1, k_lo, 1),
                    ("v", 1, 1, v_copied, 1), ("oT0", 0, 4, attn_ready, 2), ("oT1", 1, 4, attn_ready, 2),
                    ("attnT", 0, 4, attnT_lo, 1), ("xT", 1, 0, xm_high, 1), ("proj", 0, 4, y_copied, 1)]

            BANK_OF = {u[0]: u[1] for u in USES}

            def take(layer, t, name):
                at = [u[0] for u in USES].index(name)
                which = USES[at][1]
                for back in range(1, 6 * len(USES)):
                    ago, pos = divmod(at - back, len(USES))
                    user, its, behind, emptied, each = USES[pos]
                    when = t - (behind - ago)
                    if its == which and when.within(B):
                        g = in_layer(layer, when)
                        pe.wait_ge(emptied, g.count(each, 1 if user == "oT0" else each))
                        return g_bank[which]
                return g_bank[which]

            def scores(layer, g, h):
                p, blk = head_place(h)
                q, k = q_stack[p:p + ROW_MAX, g.mod(SBUFS), blk], k_stack[p:p + ROW_MAX, g.mod(SBUFS), blk]
                if h == 0:
                    pe.wait_ge(stack_loaded[g.mod(2)], g.half().count(16 * STACK_LOADS, 16 * STACK_LOADS))
                    if layer == 1:
                        first = B // 2 * 32
                        pe.wait_ge(mask_loaded[g.mod(2)], g.half().count(32, 32 - first))
                wait(pe, max_done, g.count(H, h - S_AGO[h] + 1))
                bank = s_bank[S_BANK[h]]
                if layer == 0:
                    mm(bank[:, 0:P], q[:, 0:P], k[:, 0:P], start=True, stop=False)
                    mm(bank[:, 0:P], ident16[:], tri16[:], start=False, stop=True)
                    mm(bank[:, P:3 * P], q[:, P:T], k, start=True, stop=False)
                    last = mm(bank[:, 2 * P:3 * P], ident16[:], tri16[:], start=False, stop=True)
                else:
                    for i in range(NT):
                        last = mm(bank[:, i * T:(i + 1) * T], q[:, i * P:(i + 1) * P], k, start=True, stop=True)
                last.then_inc(s_ready, 1)

            def scoresT(layer, g, h):
                p, blk = head_place(h)
                q, k = q_stack[p:p + ROWS, g.mod(SBUFS), blk], k_stack[p:p + ROWS, g.mod(SBUFS), blk]
                if h == 0:
                    pe.wait_ge(max_loaded[g.mod(2)], g.half().count(32, 32))
                wait(pe, exp_done, g.count(H, h - 1))
                bank = st_bank[h % 2]
                first = P if layer == 0 else 0
                mm(bank[:, 0:T], k[:, 0:P], q, start=True, stop=(layer == 1))
                if layer == 0:
                    mm(bank[:, 0:P], tri16[:], ident16[:], start=False, stop=True)
                last = mm(bank[:, T:2 * T - first], k[:, P:T], q[:, first:T], start=True, stop=(layer == 1))
                if layer == 0:
                    last = mm(bank[:, T:T + P], tri16[:], ident16[:], start=False, stop=True)
                last.then_inc(st_ready, 1)

            def attend(layer, g, r):
                pe.wait_ge(exp_done, g.count(H, GROUP * (r + 1)))
                if r == 0:
                    pe.wait_ge(v_copied, g.count(1, 1))
                wait(pe, o_copied, g.count(NG, r))
                first = P if layer == 0 else 0
                for kt in range(NT):
                    for j in range(GROUP):
                        h = GROUP * r + j
                        lo = first if kt else 0
                        last = mm(o_bank[32 * j:32 * j + 32, lo:T], v_sb[:, g.mod(SBUFS), kt, h, :],
                                  probs[:, h % 8, kt * T:kt * T + T - lo], start=(kt == 0), stop=(kt == NT - 1),
                                  tile_position=(0, 32 * j), skip_group_check=True)
                last.then_inc(pv_done, 1)

            def step(layer, t):
                n, a, b, c, d = (t - k for k in range(5))
                gn, ga, gb, gc, gd = (in_layer(layer, s) for s in (n, a, b, c, d))
                for s in range(H):
                    if b.within(B):
                        scores(layer, gb, s)
                    if s < LAG and d.within(B):
                        scoresT(layer, gd, s + H - LAG)
                    if s >= LAG and c.within(B):
                        scoresT(layer, gc, s - LAG)
                    if s == SLOT["xT"] and n.within(B):
                        pe.wait_ge(xn_ready, gn.count(1, 1))
                        bank = take(layer, t, "xT")
                        for f in range(NF):
                            for i in range(NT):
                                last = transpose(bank[:, f * T + i * P:f * T + (i + 1) * P],
                                                 xn[:, gn.mod(2), i, f * P:(f + 1) * P], ident[:])
                        last.then_inc(xT_ready, 1)
                    if s == SLOT["negmaxT"] and c.within(B):
                        pe.wait_ge(negmax_ready, gc.count(1, 1))
                        bank = take(layer, t, "negmaxT")
                        for i in range(NT):
                            src = negmax[:, gc.mod(2), i].bitcast(fp32).rearrange("p a b s -> p (a b s)")
                            last = transpose(bank[0:32, i * P:(i + 1) * P], src, ident[:])
                        last.then_inc(negmaxT_ready, 1)
                    for name, first, ready in (("q", 0, q_ready), ("k", D, k_ready)):
                        if s in SLOT[name] and a.within(B):
                            m = SLOT[name].index(s)
                            if m == 0:
                                bank = take(layer, t, name)
                                if name == "q":
                                    pe.wait_ge(xmT_ready, ga.count(1, 1))
                                    pe.wait_ge(wa_split, layer + 1)
                            last = project(g_bank[BANK_OF[name]], ga, first, m)
                            if m == NF - 1:
                                last.then_inc(ready, 1)
                    if s in SLOT["v"] and a.within(B):
                        i = SLOT["v"].index(s)
                        if i == 0:
                            take(layer, t, "v")
                        bank = g_bank[BANK_OF["v"]]
                        for f in range(NF):
                            last = product(bank[:, i * D:(i + 1) * D],
                                           [xmT[:, ga.mod(2), e, f, i * P:(i + 1) * P] for e in range(2)],
                                           [wa[:, e, f, 2 * D:3 * D] for e in range(2)], f, NF)
                        if i == NT - 1:
                            last.then_inc(v_ready, 1)
                    if s in SLOT["oT"] and d.within(B):
                        i = SLOT["oT"].index(s)
                        if i == 0:
                            pe.wait_ge(o_copied, gd.count(NG, NG))
                        bank = take(layer, t, f"oT{i}")
                        for r in range(NG):
                            last = transpose(bank[:, r * P:(r + 1) * P], o_sb[:, gd.mod(2), r, i * P:(i + 1) * P],
                                             ident[:])
                        last.then_inc(oT_ready, 1)
                    if s == SLOT["attnT"] and d.within(B):
                        pe.wait_ge(attn_ready, gd.count(2, 2))
                        bank = take(layer, t, "attnT")
                        for f in range(NF):
                            for i in range(NT):
                                last = transpose(bank[:, f * T + i * P:f * T + (i + 1) * P],
                                                 attn[:, i, f * P:(f + 1) * P], ident[:])
                        last.then_inc(attnT_ready, 1)
                    if s in SLOT["proj"] and d.within(B):
                        i = SLOT["proj"].index(s)
                        if i == 0:
                            pe.wait_ge(attnT_lo, gd.count(1, 1))
                            take(layer, t, "proj")
                        bank = g_bank[BANK_OF["proj"]]
                        for f in range(NF):
                            last = product(bank[:, i * D:(i + 1) * D],
                                           [attnT[:, e, f, i * P:(i + 1) * P] for e in range(2)],
                                           [wa[:, e, f, 3 * D:4 * D] for e in range(2)], f, NF)
                        if i == NT - 1:
                            last.then_inc(proj_ready, 1)
                    if s in PV_SLOT:
                        r = PV_SLOT.index(s)
                        g, on = (gc, c) if LAG + 5 + GROUP * r < H else (gd, d)
                        if on.within(B):
                            attend(layer, g, r)

            def project(bank, g, first, m):
                at = first + m * P
                for f in range(NF):
                    last = product(bank[:, m * T:(m + 1) * T], [wa[:, e, f, at:at + P] for e in range(2)],
                                   [xmT[:, g.mod(2), e, f, :] for e in range(2)], f, NF)
                return last

            def mlp_step(layer, t):
                a, b = t, t - 1
                ga, gb = (s - (-NCH * layer) for s in (a, b))
                first = b.reg is None and b.const == 0

                if b.within(NCH):
                    pe.wait_ge(m_xmT, gb.count(2, 2))
                    for m in range(NM):
                        wait(pe, m_gelu, gb.count(NM, m - 1))
                        if first:
                            pe.wait_ge(w1_split, NM * layer + m + 1)
                        for f in range(NF):
                            last = product(st_bank[m % 2][:, :], [w1[:, e, f, m * P:(m + 1) * P] for e in range(2)],
                                           [xmT_m[:, e, f, :] for e in range(2)], f, NF)
                        last.then_inc(m_h, 1)
                if a.within(NCH):
                    pe.wait_ge(m_xn, ga.count(1, 1))
                    for f in range(NF):
                        wait(pe, m_xhigh, ga.count(2, f - 1))
                        for i in range(CT):
                            last = transpose(s_bank[f][:, i * P:(i + 1) * P],
                                             xn_m[:, i, f * P:(f + 1) * P], ident[:])
                        last.then_inc(m_xT, 1)
                if b.within(NCH):
                    for i in range(2):
                        wait(pe, m_ycopied, gb.count(2, i - 1))
                        for k in range(NT):
                            at = (NT * i + k) * P
                            for m in range(NM):
                                if i == 0 and k == 0:
                                    pe.wait_ge(m_hT, gb.count(NM, m + 1))
                                    if first:
                                        pe.wait_ge(w2_split, NM * layer + m + 1)
                                last = product(g_bank[i][:, k * D:(k + 1) * D],
                                               [hT[:, e, m, at:at + P] for e in range(2)],
                                               [w2[:, e, m, :] for e in range(2)], m, NM)
                        last.then_inc(m_y, 1)

            pe.wait_ge(setup_done, 1)
            for layer in range(LAYERS):
                if layer:
                    pe.wait_ge(m_ycopied, 2 * NCH)
                for t in steps(pe, B, 4, 5, 4):
                    if layer == 0 and t.reg is None and t.const == 1:
                        set_up_layer1()
                    if t.reg is None and t.const == 2:
                        pe.wait_ge(rows_set, 96 + 64 * layer)
                    if t.reg is None and t.const == 3:
                        pe.wait_ge(vones_set, layer + 1)
                    step(layer, t)
                pe.wait_ge(y_copied, B * (layer + 1))
                for t in steps(pe, NCH, 2, 2, 2):
                    mlp_step(layer, t)

        @block.scalar
        def _(act):
            activation = nc.scalar.activation
            act.wait_ge(vec_loaded, 16 * VEC_LOADS)
            activation(sig, cond, ACT.Exp, scale=-1.0).then_inc(expneg, 1)
            act.wait_ge(setup_done, 1)
            cq = COLS["bqk"][0]

            def step(layer, t):
                n, a, c, d = t, t - 1, t - 3, t - 4
                gn, ga, gc, gd = (in_layer(layer, s) for s in (n, a, c, d))

                def exponentials(g, h):
                    act.wait_ge(st_ready, g.count(H, h + 1))
                    wait(act, pv_done, g.count(NG, h // GROUP - 1))
                    n = 3 * P if layer == 0 else 4 * P
                    activation(probs[:, h % 8, 0:n], st_bank[h % 2][:, 0:n], ACT.Exp, scale=SCALE)\
                        .then_inc(exp_done, 1)

                def outputs(g, r):
                    act.wait_ge(pv_done, g.count(NG, r + 1))
                    if r == 0:
                        wait(act, oT_ready, g.count(2, -2))
                    activation(o_sb[:, g.mod(2), r, :], o_bank[:, 0:T], ACT.Copy).then_inc(o_copied, 1)

                def high(ready, done, stored, bank, split, first):
                    act.wait_ge(ready, ga.count(1, 1))
                    wait(act, stored, ga.count(16))
                    if layer == 0:
                        activation(split[:, 0], bank[:].rearrange("p (f n) -> p f n", f=NF), ACT.Copy)\
                            .then_inc(done, 1)
                    else:
                        for f in range(NF):
                            last = activation(split[:, 0, f], bank[:, f * T:(f + 1) * T], ACT.Identity,
                                              bias=cols[:, cq + first + f:cq + first + f + 1])
                        last.then_inc(done, 1)

                for s in range(H):
                    if s < LAG and d.within(B):
                        exponentials(gd, s + H - LAG)
                    if s >= LAG and c.within(B):
                        exponentials(gc, s - LAG)
                    if s == SLOT["negmaxT"] and c.within(B):
                        act.wait_ge(negmaxT_ready, gc.count(1, 1))
                        last_batch = gc - 1
                        wait(act, max_loaded[last_batch.mod(2)], last_batch.half().count(32, 32)
                             if c.reg is not None or c.const + layer else None)
                        activation(negmaxT[:], g_bank[0][0:32, 0:T], ACT.Copy).then_inc(negmaxT_copied, 1)
                    if s == SLOT["q"][1] and a.within(B):
                        high(q_ready, q_hi, q_stored, g_bank[1], q_split, 0)
                    if s == SLOT["k"][1] and a.within(B):
                        high(k_ready, k_hi, k_stored, g_bank[0], k_split, NF)
                    if s == SLOT["v"][1] and a.within(B):
                        act.wait_ge(v_ready, ga.count(1, 1))
                        wait(act, pv_done, ga.count(NG, NG - SBUFS * NG))
                        activation(v_sb[:, ga.mod(SBUFS), :, :, 0:HD],
                                   g_bank[1][:].rearrange("p (i h d) -> p i h d", i=NT, h=H), ACT.Copy)\
                            .then_inc(v_copied, 1)
                    if s == SLOT["attnT"] and d.within(B):
                        act.wait_ge(attnT_ready, gd.count(1, 1))
                        wait(act, proj_ready, gd.count(1))
                        activation(attnT[:, 0], g_bank[0][:].rearrange("p (f n) -> p f n", f=NF), ACT.Copy)\
                            .then_inc(attnT_hi, 1)
                    if s in (SLOT["xT"], SLOT["xT"] + 1) and n.within(B):
                        f = s - SLOT["xT"]
                        if f == 0:
                            act.wait_ge(xT_ready, gn.count(1, 1))
                            wait(act, v_ready, gn.count(1, -1))
                            wait(act, xmT_ready, gn.count(1))
                        for dst in (xm_full, xmT[:, gn.mod(2), 0]):
                            last = activation(dst[:, f], g_bank[1][:, f * T:(f + 1) * T], ACT.Identity,
                                              scale=tab(layer, A1, f, n), bias=tab(layer, B1, f, n))
                        if f == NF - 1:
                            last.then_inc(xm_high, 1)
                    if s in PV_SLOT:
                        r = PV_SLOT.index(s)
                        g, on = (gc, c) if LAG + 5 + GROUP * r < H else (gd, d)
                        if on.within(B):
                            outputs(g, r)

            def mlp_step(layer, t):
                a, b = t, t - 1
                ga, gb = (s - (-NCH * layer) for s in (a, b))

                def modulate(dst, src, f, scale, shift, chunk):
                    for k in range(2):
                        batch = Step(chunk.const * 2 + k, chunk.reg, chunk.stride * 2)
                        last = activation(dst[:, k * T:(k + 1) * T], src[:, k * T:(k + 1) * T], ACT.Identity,
                                          scale=tab(layer, scale, f, batch), bias=tab(layer, shift, f, batch))
                    return last

                if b.within(NCH):
                    cb = COLS[f"b1_{layer}"][0]
                    for m in range(NM):
                        act.wait_ge(m_h, gb.count(NM, m + 1))
                        wait(act, m_hT, gb.count(NM, m - 1))
                        activation(h_full[:, m % 2], st_bank[m % 2][:, :], ACT.Gelu, bias=cols[:, cb + m:cb + m + 1])\
                            .then_inc(m_gelu, 1)
                if a.within(NCH):
                    for f in range(NF):
                        act.wait_ge(m_xT, ga.count(2, f + 1))
                        wait(act, m_xmT, ga.count(2, f - 1))
                        modulate(xm_full_m[:, f], s_bank[f], f, A2, B2, a)
                        modulate(xmT_m[:, 0, f], s_bank[f], f, A2, B2, a).then_inc(m_xhigh, 1)

            for layer in range(LAYERS):
                if layer:
                    act.wait_ge(m_h, NM * NCH * layer)
                for t in steps(act, B, 4, 5, 4):
                    if t.reg is None and t.const == 1 and layer == 0:
                        act.wait_ge(setup_done, 2)
                        act.wait_ge(vones_set, 1)
                    if t.reg is None and t.const == 1 and layer == 1:
                        act.wait_ge(vones_set, 2)
                    if t.reg is None and t.const == 3:
                        act.wait_ge(mask_stored, 16)
                        act.wait_ge(rows_set, 96 + 64 * layer)
                        wait(act, m_added, 2 * NCH * layer or None)
                        wait(act, m_hT, NM * NCH * layer or None)
                    step(layer, t)
                act.wait_ge(pv_done, NG * B * (layer + 1))
                act.wait_ge(st_ready, H * B * (layer + 1))
                act.wait_ge(wm_loaded, 32 * (layer + 1))
                for m in range(NM):
                    activation(w2[:, 0, m], w2_raw[:, m], ACT.Copy).then_inc(w2_high, 1)
                for t in steps(act, NCH, 2, 2, 2):
                    mlp_step(layer, t)

        @block.vector
        def _(dve):
            v = nc.vector
            links = [0]

            def link(ins):
                links[0] += 1
                ins.then_inc(chain, 1)
                dve.wait_ge(chain, links[0])

            def set_ones():
                v.memset(ones.bitcast(fp32), 1.0).then_inc(ones_set, 1)
                v.memset(zeros.bitcast(fp32), 0.0).then_inc(ones_set, 1)

            def split(dst, src, high, last_high, low):
                v.tensor_copy(dst[0], src).then_inc(high, 1)
                dve.wait_ge(high, last_high)
                v.tensor_tensor(dst[1], src, dst[0], ALU.subtract).then_inc(low, 1)

            def split_attention_weights(layer):
                dve.wait_ge(wa_loaded, 16 * (layer + 1))
                split([wa[:, e] for e in range(2)], wa_raw[layer], wa_high, layer + 1, wa_split)

            def split_w1(layer):
                dve.wait_ge(wm_loaded, 32 * (layer + 1))
                for m in range(NM):
                    at = slice(m * P, (m + 1) * P)
                    split([w1[:, e, :, at] for e in range(2)], w1_raw[:, :, at], w1_high, NM * layer + m + 1,
                          w1_split)

            def col(name, n, first=0):
                at = COLS[name][0] + first
                return cols[:, at:at + n].unsqueeze(2).to_broadcast((P, n, B))

            def kind(layer, k):
                return table[layer][:, k * NF * B:(k + 1) * NF * B].rearrange("p (f b) -> p f b", f=NF)

            def set_up_layer0():
                dve.wait_ge(vec_loaded, 16 * VEC_LOADS)
                dve.wait_ge(expneg, 1)
                link(v.tensor_scalar(sig, sig, 1.0, None, ALU.add))
                link(v.reciprocal(sig, sig))
                v.tensor_tensor(silu, sig, cond, ALU.mult).then_inc(silu_ready, 1)
                dve.wait_ge(mods_ready, 1)
                for n, part in enumerate(COLUMN_PARTS):
                    at = slice(n * NF, (n + 1) * NF)
                    last = v.tensor_tensor(mod0[:, at], g_bank[0][:].rearrange("p (j b) -> p j b", b=B)[:, at],
                                           col("bada", NF, part * NF), ALU.add)
                link(last)
                for n, ka, kb, g, be in ((0, A1, B1, "g1", "be1"), (2, A2, B2, "g2", "be2")):
                    shift, scale = (mod0[:, i * NF:(i + 1) * NF] for i in (n, n + 1))
                    v.scalar_tensor_tensor(out=kind(0, ka), in0=scale, scalar=1.0, in1=col(g, NF), op0=ALU.add,
                                           op1=ALU.mult)
                    link(v.scalar_tensor_tensor(out=kind(0, kb), in0=scale, scalar=1.0, in1=col(be, NF),
                                                op0=ALU.add, op1=ALU.mult))
                    last = v.tensor_tensor(kind(0, kb), kind(0, kb), shift, ALU.add)
                last.then_inc(setup_done, 1)
                v.tensor_tensor(gates, g_bank[1][0:B, :], gates, ALU.add).then_inc(gates_ready, 1)

            def set_up_layer1():
                c0 = COLS["bv"][0]
                dve.wait_ge(late_loaded, 16 * LATE_LOADS)
                v.tensor_copy(bv_wide, cols[:, c0:c0 + NF].unsqueeze(2).to_broadcast((P, NF, P)))\
                    .then_inc(bv_spread, 1)
                v.tensor_copy(ident16[:], ident[:])
                v.tensor_copy(tri16[:], tri)
                v.tensor_scalar(maskf, mask_int, BIG, None, ALU.mult).then_inc(maskf_ready, 1)
                dve.wait_ge(mods_ready, 2)
                link(v.tensor_tensor(mod1, s_bank[0][:, 0:4 * NF * B].rearrange("p (j b) -> p j b", b=B),
                                     col("bada1", 4 * NF), ALU.add))
                for first, ka, kb in ((0, A1, B1), (2, A2, B2)):
                    v.tensor_scalar(kind(1, ka), mod1[:, first * NF:(first + 1) * NF], 1.0, None, ALU.add)
                    v.tensor_copy(kind(1, kb), mod1[:, (first + 1) * NF:(first + 2) * NF])
                v.tensor_tensor(bias_rows[:, 1], s_bank[1][:, 0:D], bias_rows[:, 1], ALU.add)\
                    .then_inc(setup_done, 1)

            def statistics(rows, tiles, into, mean_var, part, done, g, used):
                wait(dve, used[0], used[1])
                for i in range(tiles):
                    v.bn_stats(into[:, i, :], rows[:, i * D:(i + 1) * D]).then_inc(part, 1)
                wait_apart(dve, part, g.count(tiles, tiles), dve_passed)
                for i in range(tiles):
                    last = v.bn_aggr(mean_var[:, i, :], into[:, i, :])
                last.then_inc(done, 1)

            def normalise(rows, tiles, dst, mean_var, rs, rdy, done, g):
                dve.wait_ge(rdy, g.count(1, 1))
                for i in tiles:
                    last = v.tensor_scalar(dst[:, i, :], rows[:, i * D:(i + 1) * D], mean_var[:, i, 0:1],
                                           rs[:, i:i + 1], ALU.subtract, ALU.mult)
                if done is not None:
                    last.then_inc(done, 1)

            def low(layer, g, ready, done, bank, split, first):
                dve.wait_ge(ready, g.count(1, 1))
                c = COLS["bqk"][0] + first
                if layer == 0:
                    v.tensor_tensor(split[:, 1], bank[:].rearrange("p (f n) -> p f n", f=NF), split[:, 0],
                                    ALU.subtract).then_inc(done, 1)
                else:
                    for f in range(NF):
                        last = v.scalar_tensor_tensor(out=split[:, 1, f], in0=bank[:, f * T:(f + 1) * T],
                                                      scalar=cols[:, c + f:c + f + 1], in1=split[:, 0, f],
                                                      op0=ALU.add, op1=ALU.subtract)
                    last.then_inc(done, 1)

            def step(layer, t):
                n, a, b, d = t, t - 1, t - 2, t - 4
                gn, ga, gb, gd = (in_layer(layer, s) for s in (n, a, b, d))
                last_step = t.reg is None and t.const == B + 3
                for s in range(H):
                    if b.within(B):
                        if s == 0:
                            wait(dve, negmax_ready, gb.count(1, -1))
                        dve.wait_ge(s_ready, gb.count(H, s + 1))
                        bank = s_bank[S_BANK[s]]
                        if layer == 0:
                            v.reduce_max(maxima[:, gb.mod(2), s, 0:3],
                                         bank[:, 0:3 * P].rearrange("p (i n) -> p i n", n=P), AX.X)\
                                .then_inc(max_done, 1)
                        else:
                            v.reduce_max(maxima[:, gb.mod(2), s, 0:2],
                                         bank[:].rearrange("p (i n) -> p i n", n=T), AX.X).then_inc(max_done, 1)
                    if s == SLOT["q"][1] and a.within(B):
                        low(layer, ga, q_hi, q_lo, g_bank[1], q_split, 0)
                    if s == 3 and n.within(B):
                        if n.reg is None:
                            dve.wait_ge(x_loaded[n.const // 4], 16)
                        elif layer == 0 and n.const == 4:
                            for i in range(1, 4):
                                dve.wait_ge(x_loaded[i], 16)
                        if layer:
                            dve.wait_ge(m_added, n.count(1, 1))
                        statistics(xrows(n, NT), NT, stats[:, gn.mod(2)], mv[:, gn.mod(2)], stats_part, mv_ready, gn,
                                   (xn_ready, gn.count(1, -1)))
                    if s == SLOT["k"][1] and a.within(B):
                        low(layer, ga, k_hi, k_lo, g_bank[0], k_split, NF)
                    if s == 7 and n.within(B):
                        wait(dve, xT_ready, gn.count(1, -1))
                        normalise(xrows(n, NT), range(NT), xn[:, gn.mod(2)], mv[:, gn.mod(2)], rstd[:, gn.mod(2)],
                                  rstd_ready, xn_ready, gn)
                    if s in SLOT["oT"] and d.within(B):
                        i = SLOT["oT"].index(s)
                        dve.wait_ge(oT_ready, gd.count(2, i + 1))
                        if i == 0:
                            wait(dve, attnT_ready, gd.count(1))
                            if layer == 0 and d.const == 0:
                                dve.wait_ge(gates_stored, 16)
                        o = g_bank[i][:].rearrange("p (h n) -> p h n", n=32)
                        wait(dve, attn_ready, gd.count(2, i))
                        v.reciprocal(rsum[:, i], o[:, :, HD]).then_inc(rsum_ready, 1)
                        dve.wait_ge(rsum_ready, gd.count(2, i + 1))
                        v.tensor_tensor(attn[:, i].rearrange("p (h n) -> p h n", n=HD), o[:, :, 0:HD],
                                        rsum[:, i].unsqueeze(2).to_broadcast((P, H, HD)), ALU.mult)\
                            .then_inc(attn_ready, 1)
                    if s == SLOT["attnT"] and d.within(B):
                        dve.wait_ge(attnT_hi, gd.count(1, 1))
                        v.tensor_tensor(attnT[:, 1], g_bank[0][:].rearrange("p (f n) -> p f n", f=NF), attnT[:, 0],
                                        ALU.subtract).then_inc(attnT_lo, 1)
                    if s == SLOT["proj"][1] and d.within(B):
                        dve.wait_ge(proj_ready, gd.count(1, 1))
                        wait(dve, x_added, gd.count(1))
                        v.tensor_tensor(y_sb[:], g_bank[0][:].rearrange("p (i n) -> p i n", i=NT),
                                        bias_rows[:, layer].unsqueeze(1).to_broadcast((P, NT, D)), ALU.add)\
                            .then_inc(y_copied, 1)
                    if last_step and s == SLOT["k"][1]:
                        chunk_statistics(layer, Step(0))
                    if last_step and s == SLOT["attnT"]:
                        chunk_normalise(layer, Step(0), range(CT))
                if b.within(B):
                    m = maxima[:, gb.mod(2)]
                    dve.wait_ge(max_done, gb.count(H, H))
                    if layer == 0:
                        v.tensor_tensor(m[:, :, 1], m[:, :, 1], m[:, :, 2], ALU.max).then_inc(max_joined, 1)
                        dve.wait_ge(max_joined, gb.count(1, 1))
                    wait(dve, negmaxT_ready, gb.count(1, -1))
                    for i in range(NT):
                        src = m[:, :, i].rearrange("p (f j e) -> p e j f", f=2, e=2)
                        dst = negmax[:, gb.mod(2), i].rearrange("p e c (j f) -> p e c j f", f=2)
                        last = v.tensor_scalar(dst[:, :, 0], src, -1.0, None, ALU.mult)
                    last.then_inc(negmax_hi, 1)
                    dve.wait_ge(negmax_hi, gb.count(1, 1))
                    for i in range(NT):
                        src = m[:, :, i].rearrange("p (f j e) -> p e j f", f=2, e=2)
                        dst = negmax[:, gb.mod(2), i].rearrange("p e c (j f) -> p e c j f", f=2)
                        for e in range(2):
                            last = v.scalar_tensor_tensor(out=dst[:, e, 1], in0=src[:, e], scalar=-1.0,
                                                          in1=dst[:, e, 0], op0=ALU.mult, op1=ALU.subtract)
                    last.then_inc(negmax_ready, 1)

            def chunk_rows(chunk):
                return xrows(Step(chunk.const * 2, chunk.reg, chunk.stride * 2), CT)

            def chunk_statistics(layer, a):
                ga = a - (-NCH * layer)
                dve.wait_ge(x_added, ga.count(2, 2))
                statistics(chunk_rows(a), CT, stats_m, mv_m, m_stats, m_mv, ga, (m_xn, ga.count(1)))

            def chunk_normalise(layer, a, tiles):
                ga = a - (-NCH * layer)
                if tiles[0] == 0:
                    if a.reg is None and a.const == 0:
                        dve.wait_ge(xT_ready, B * (layer + 1))
                    wait(dve, m_xT, ga.count(2))
                normalise(chunk_rows(a), tiles, xn_m, mv_m, rstd_m, m_rstd, m_xn if tiles[-1] == CT - 1 else None,
                          ga)

            def mlp_step(layer, t):
                a, b = t, t - 1
                ga, gb = (s - (-NCH * layer) for s in (a, b))
                if a.within(NCH) and not (t.reg is None and t.const == 0):
                    chunk_statistics(layer, a)
                if t.reg is None and t.const == 0:
                    dve.wait_ge(st_ready, B * H * (layer + 1))
                    split_w1(layer)
                if b.within(NCH):
                    for m in range(NM):
                        dve.wait_ge(m_gelu, gb.count(NM, m + 1))
                        if m == 0:
                            wait(dve, m_y, gb.count(2))
                        v.tensor_copy(hT[:, 0, m], h_full[:, m % 2]).then_inc(m_hhigh, 1)
                        dve.wait_ge(m_hhigh, gb.count(NM, m + 1))
                        v.tensor_tensor(hT[:, 1, m], h_full[:, m % 2], hT[:, 0, m], ALU.subtract).then_inc(m_hT, 1)
                        if a.within(NCH) and m in (3, 5):
                            chunk_normalise(layer, a, range(m - 3, m - 1))
                if a.within(NCH):
                    for f in range(NF):
                        dve.wait_ge(m_xhigh, ga.count(2, f + 1))
                        v.tensor_tensor(xmT_m[:, 1, f], xm_full_m[:, f], xmT_m[:, 0, f], ALU.subtract)\
                            .then_inc(m_xmT, 1)
                if b.within(NCH):
                    for i in range(2):
                        dve.wait_ge(m_y, gb.count(2, i + 1))
                        wait(dve, m_added, gb.count(2, i - 1))
                        if b.reg is None and b.const == 0 and i == 0:
                            dve.wait_ge(bias_loaded, 16 * (layer + 1))
                        v.tensor_tensor(y_m[:, i], g_bank[i][:].rearrange("p (i n) -> p i n", i=NT),
                                        bias_rows[:, 0].unsqueeze(1).to_broadcast((P, NT, D)), ALU.add)\
                            .then_inc(m_ycopied, 1)
                if layer == 0 and t.reg is None and t.const == 1:
                    split_attention_weights(1)

            set_ones()
            set_up_layer0()
            for layer in range(LAYERS):
                for t in steps(dve, B, 4, 5, 4):
                    if layer == 0 and t.reg is None and t.const == 1:
                        split_attention_weights(0)
                        set_up_layer1()
                    step(layer, t)
                if layer == 0:
                    dve.wait_ge(proj_ready, B)
                    set_ones()
                for t in steps(dve, NCH, 2, 2, 2):
                    mlp_step(layer, t)

        @block.gpsimd
        def _(pool):
            g_ = nc.gpsimd

            g_.memset(half_power[:], -0.5).then_inc(power_set, 1)
            pool.wait_ge(power_set, 1)

            def inverse_deviation(dst, var, tiles, shifted, g, done):
                g_.tensor_scalar(dst, var, EPS, 1.0, ALU.add, ALU.mult).then_inc(shifted, 1)
                pool.wait_ge(shifted, g.count(1, 1))
                g_.tensor_tensor(dst, dst, half_power[:, 0:tiles], ALU.pow).then_inc(done, 1)

            def output(layer, y, rows, gate, copied, done):
                pool.wait_ge(*copied)
                if layer == 0:
                    pool.wait_ge(gate_loaded[gate[0]], gate[1])
                    g_.tensor_tensor(y, y, gate_rows[:, gate[0]].unsqueeze(1).to_broadcast((P, NT, D)), ALU.mult)\
                        .then_inc(y_gated, 1)
                    pool.wait_ge(y_gated, gate[2])
                g_.tensor_tensor(rows.rearrange("p (i n) -> p i n", i=NT), rows.rearrange("p (i n) -> p i n", i=NT),
                                 y, ALU.add).then_inc(done, 1)

            def chunk_deviation(layer, a):
                g = a - (-NCH * layer)
                wait_apart(pool, m_mv, g.count(1, 1), pool_passed)
                inverse_deviation(rstd_m[:], mv_m[:, :, 1], CT, m_shifted, g, m_rstd)

            def step(layer, t):
                n, d = t, t - 4
                gn, gd = in_layer(layer, n), in_layer(layer, d)
                if n.within(B):
                    wait_apart(pool, mv_ready, gn.count(1, 1), pool_passed)
                    inverse_deviation(rstd[:, gn.mod(2)], mv[:, gn.mod(2), :, 1], NT, var_shifted, gn, rstd_ready)
                    pool.wait_ge(xm_high, gn.count(1, 1))
                    g_.tensor_tensor(xmT[:, gn.mod(2), 1], xm_full[:], xmT[:, gn.mod(2), 0], ALU.subtract)\
                        .then_inc(xmT_ready, 1)
                if t.reg is None and t.const == B + 3:
                    chunk_deviation(layer, Step(0))
                if d.within(B):
                    output(layer, y_sb[:], xrows(d, NT), (gd.mod(2), gd.half().count(16, 16), gd.count(1, 1)),
                           (y_copied, gd.count(1, 1)), x_added)

            def mlp_step(layer, t):
                a, b = t, t - 1
                gb = b - (-NCH * layer)
                if t.reg is None and t.const == 0:
                    for m in range(NM):
                        done = NM * layer + m + 1
                        pool.wait_ge(w2_high, done)
                        g_.tensor_tensor(w2[:, 1, m], w2_raw[:, m], w2[:, 0, m], ALU.subtract).then_inc(w2_split, 1)
                elif a.within(NCH):
                    chunk_deviation(layer, a)
                if b.within(NCH):
                    for i in range(2):
                        batch = Step(b.const * 2 + i, b.reg, b.stride * 2)
                        output(layer, y_m[:, i], xrows(batch, NT),
                               (i, b.count(16, 16 * (B // 2) + 16), batch.count(1, B + 1)),
                               (m_ycopied, gb.count(2, i + 1)), m_added)

            for layer in range(LAYERS):
                for t in steps(pool, B, 4, 5, 4):
                    if t.reg is None and t.const == 1:
                        pool.wait_ge(wa_split, layer + 1)
                        pool.wait_ge(setup_done, 2)
                        g_.memset(v_sb[:, :, :, :, HD:32], 1.0).then_inc(vones_set, 1)
                    step(layer, t)
                for t in steps(pool, NCH, 2, 2, 2):
                    mlp_step(layer, t)


def kernel(**inputs):
    import numpy as np
    import concourse.bacc as bacc
    from concourse.bass_utils import run_bass_kernel_spmd

    a = {k: np.asarray(v) for k, v in inputs.items()}

    def rows(w):
        return np.ascontiguousarray(w.reshape(-1, P, w.shape[1]).transpose(1, 0, 2))

    def columns(v):
        return v.reshape(-1, P).T

    order = np.array([((4 * t + i) * 2 + par) * HD + d
                      for t in range(NF) for par in range(2) for d in range(HD) for i in range(4)])
    wqkv0 = a["L0_cond_Wqkv"]
    q0, k0, v0 = wqkv0[:, 0:D], wqkv0[:, D:2 * D], wqkv0[:, 2 * D:]
    q1, k1, v1 = a["L1_cond_wq"].T, a["L1_cond_wk"].T, a["L1_cond_wv"].T
    vectors = {"g1": a["L0_cond_g1"], "be1": a["L0_cond_be1"], "g2": a["L0_cond_g2"], "be2": a["L0_cond_be2"],
               "b1_0": a["L0_cond_b1"],
               "bada": a["L0_cond_bada"], "bada1": np.concatenate([a["L1_cond_b_adaln1"], a["L1_cond_b_adaln2"]]),
               "bqk": np.concatenate([a["L1_cond_bq"][order], a["L1_cond_bk"][order]]), "bv": a["L1_cond_bv"],
               "b1_1": a["L1_cond_b1"]}
    bada = a["L0_cond_bada"]
    rows_of = {"bproj": a["L0_cond_bproj"], "b2_0": a["L0_cond_b2"], "bo": a["L1_cond_bo"], "b2_1": a["L1_cond_b2"],
               "gate_attn": bada[2 * D:3 * D], "gate_mlp": bada[5 * D:6 * D]}
    mask_words = np.zeros((B, T, 4), np.uint8)
    mask_words[:, :, 0] = a["mask_BxS_bf0"].view(np.uint8)
    arrays = {
        "x_in": a["x"].reshape(B * T, D),
        "cond_in": rows(a["cond_1024"].T),
        "mask_in": mask_words.view(np.int32)[:, :, 0],
        "wa_in": np.stack([rows(np.concatenate([q0[:, order], k0[:, order], v0, a["L0_cond_Wproj"]], axis=1)),
                           rows(np.concatenate([q1[:, order], k1[:, order], v1, a["L1_cond_wo"].T], axis=1))]),
        "w1_in": np.stack([rows(a["L0_cond_W1"]), rows(a["L1_cond_w1"].T)]),
        "w2_in": np.stack([rows(a["L0_cond_W2"]), rows(a["L1_cond_w2"].T)]),
        "ada0_in": rows(a["L0_cond_Wada"]),
        "ada1_in": rows(np.concatenate([a["L1_cond_w_adaln1"].T, a["L1_cond_w_adaln2"].T], axis=1)),
        "cols_in": np.concatenate([columns(vectors[name]) for name in COLS], axis=1),
        "rows_in": np.stack([rows_of[name] for name in ROWS_IN]),
        "ident_in": np.eye(P, dtype=np.float32),
        "tri_in": np.where(np.arange(P)[None, :] > np.arange(P)[:, None], BIG, 0.0).astype(np.float32),
    }
    nc = bacc.Bacc("TRN2", target_bir_lowering=False, num_devices=1)
    args = []
    for name in arrays:
        arrays[name] = np.ascontiguousarray(arrays[name])
        args.append(nc.dram_tensor(name, arrays[name].shape, mybir.dt.from_np(arrays[name].dtype),
                                   kind="ExternalInput").ap())
    out = nc.dram_tensor("out", (B * T, D), mybir.dt.float32, kind="ExternalOutput").ap()
    build(nc, *args, out)
    r = run_bass_kernel_spmd(nc, [arrays], core_ids=[0])
    return r.results[0]["out"].reshape(B, T, D)
```

```python
import concourse.bass as bass
from concourse import mybir
from contextlib import ExitStack

LAYERS, B, T, D = 2, 16, 256, 256
H, HD = 16, 16
F = 4 * D
P = 128
NF, NM, NT = D // P, F // P, T // P
EPS = 1e-5
SCALE = HD ** -0.5
BIG = -1e30
GROUP = 4
NG = H // GROUP
SLOTS = H // 2
SBUFS = 4
LAG = 5
S_BANK = [h % 3 for h in range(H - 1)] + [1]
S_AGO = [next(k for k in range(1, H) if S_BANK[h - k] == S_BANK[h]) for h in range(H)]
SLOT = {"q": (0, 1), "negmaxT": 1, "k": (3, 5), "v": (6, 7), "oT": (8, 9), "attnT": 11, "xT": 12, "proj": (14, 15)}
PV_SLOT = [(LAG + 5 + GROUP * i) % H for i in range(NG)]
ROW_MASK, ROW_MAX, ROWS = 3 * HD, 3 * HD + 1, 3 * HD + 3

COLS, _at = {}, 0
for _name, _n in [("g1", NF), ("be1", NF), ("g2", NF), ("be2", NF), ("b1_0", NM),
                  ("bada", 6 * NF), ("bada1", 4 * NF), ("bqk", 2 * NF), ("bv", NF), ("b1_1", NM)]:
    COLS[_name] = (_at, _n)
    _at += _n
NCOLS = _at
A1, B1, A2, B2 = KINDS = range(4)
COLUMN_PARTS, GATE_PARTS = (0, 1, 3, 4), (2, 5)
ROWS_IN = ["bproj", "b2_0", "bo", "b2_1", "gate_attn", "gate_mlp"]


class Step:

    def __init__(self, const, reg=None, stride=0):
        self.const, self.reg, self.stride = const, reg, stride

    def __sub__(self, k):
        return Step(self.const - k, self.reg, self.stride)

    def within(self, n):
        return self.reg is not None or 0 <= self.const < n

    def mod(self, m):
        return self.const % m

    def half(self):
        return Step(self.const // 2, self.reg, self.stride // 2)

    def count(self, each, plus=0):
        v = self.const * each + plus
        if self.reg is not None:
            return self.reg * (self.stride * each) + v
        return v if v > 0 else None


def wait(eng, sem, value):
    if value is not None:
        eng.wait_ge(sem, value)


def wait_apart(eng, sem, value, passed):
    if value is not None:
        eng.wait_ge(sem, value)
        eng.sem_inc(passed, 1)


def steps(eng, n, start, first, stages, unroll):
    last = n + stages - 1
    turns = (n - first) // unroll
    for t in range(start, first):
        yield Step(t)
    with eng.Fori(0, turns) as i:
        for u in range(unroll):
            yield Step(first + u, i, unroll)
    for t in range(first + turns * unroll, last):
        yield Step(t)


def head_place(h):
    pair, parity = h // 2, h % 2
    tile, i = pair // 4, pair % 4
    return 64 * parity, i * NF + tile


def build(nc, x_in, cond_in, mask_in, wa_in, w1_in, w2_in, ada0_in, ada1_in, cols_in, rows_in, ident_in,
          tri_in, out):
    fp32, f32r, bf16 = mybir.dt.float32, mybir.dt.float32r, mybir.dt.bfloat16
    ALU, ACT, AX = mybir.AluOpType, mybir.ActivationFunctionType, mybir.AxisListType

    with ExitStack() as ctx:
        def sb(name, shape, dt=fp32):
            return ctx.enter_context(nc.sbuf_tensor(name, shape, dt))

        def bank(name):
            return ctx.enter_context(nc.psum_tensor(name, [P, 512], fp32))

        def sem(name):
            return ctx.enter_context(nc.semaphore(name))

        x_sb = sb("x_sb", [P, B * NT * D])
        wa = sb("wa", [P, 2, NF, 4 * D], f32r)
        wm_raw = sb("wm_raw", [P, NF * F + NM * D])
        cols = sb("cols", [P, NCOLS])
        ident = sb("ident", [P, P])
        ident16 = sb("ident16", [P, P], bf16)
        tri16 = sb("tri16", [P, P], bf16)
        table = [sb(f"table{l}", [P, len(KINDS) * NF * B]) for l in range(LAYERS)]
        q_stack = sb("q_stack", [P, SBUFS, SLOTS, T], f32r)
        k_stack = sb("k_stack", [P, SBUFS, SLOTS, T], f32r)
        v_sb = sb("v_sb", [P, SBUFS, NT, H, 32])
        probs = sb("probs", [P, 8, 512])
        stats = sb("stats", [P, 2, NT, 6])
        mv = sb("mv", [P, 2, NT, 2])
        rstd = sb("rstd", [P, 2, NT])
        xn = sb("xn", [P, 2, NT, D])
        xm_full = sb("xm_full", [P, NF, T])
        xmT = sb("xmT", [P, 2, 2, NF, T], f32r)
        qk_split = sb("qk_split", [P, 2, 2, NF, T], f32r)
        q_split, k_split = qk_split[:, 0], qk_split[:, 1]
        maxima = sb("maxima", [P, 2, H, 3])
        negmax = sb("negmax", [P, 2, NT, 2, 2, SLOTS], f32r)
        negmaxT = sb("negmaxT", [32, T], f32r)
        o_sb = sb("o_sb", [P, 2, NG, T])
        rsum = sb("rsum", [P, 2, H])
        attn = sb("attn", [P, NT, D])
        attnT = sb("attnT", [P, 2, NF, T], f32r)
        y_sb = sb("y_sb", [P, NT, D])
        bias_rows = sb("bias_rows", [P, 2, D])
        gate_rows = sb("gate_rows", [P, 2, D])

        CH = 2 * T
        CT = CH // P
        v_flat = v_sb[:].rearrange("p a t h n -> p (a t h n)")
        o_flat = o_sb[:].rearrange("p a g n -> p (a g n)")
        maskf = negmaxT[0:B]
        xn_flat = xn[:].rearrange("p a t n -> p (a t n)")
        probs_flat = probs[:].rearrange("p a n -> p (a n)")
        free = NF * 4 * D

        def in_probs(n):
            nonlocal free
            free += n
            return probs_flat[:, free - n:free]

        cond, silu, sig, mod0, mod1 = (in_probs(n * B).rearrange("p (j b) -> p j b", b=B)
                                       for n in (NF, NF, NF, len(COLUMN_PARTS) * NF, 4 * NF))
        tri = in_probs(P)
        mask_int = in_probs(T)[0:B].bitcast(mybir.dt.int32)
        bv_wide = in_probs(NF * P).rearrange("p (f n) -> p f n", f=NF)
        gates = attn[0:B].rearrange("p i n -> p (i n)")
        ones_zeros = attnT[:].rearrange("p a f n -> p (a f n)")
        ones, zeros = ones_zeros[0:16], ones_zeros[32:40]
        ada0 = wm_raw[:, 0:NF * 6 * D].rearrange("p (f n) -> p f n", f=NF)
        ada1 = probs_flat[:, 0:NF * 4 * D].rearrange("p (f n) -> p f n", f=NF)
        wa_raw = [w[:, 0:NF * 4 * D].rearrange("p (f n) -> p f n", f=NF) for w in (o_flat, v_flat)]
        wo_raw = y_sb[:]
        w1_raw = wm_raw[:, 0:NF * F].rearrange("p (f n) -> p f n", f=NF)
        w2_raw = wm_raw[:, NF * F:].rearrange("p (m n) -> p m n", m=NM)
        q_flat = q_stack[:].rearrange("p a s n -> p (a s n)")
        w1 = q_flat[:, 0:2 * NF * F].rearrange("p (a f n) -> p a f n", a=2, f=NF)
        w2 = q_flat[:, 2 * NF * F:].rearrange("p (a m n) -> p a m n", a=2, m=NM)
        hT = k_stack[:].rearrange("p a s n -> p (a s n)").rearrange("p (i a m n) -> p i a m n", i=2, a=2, m=NM)
        h_full = probs[:, 0:2]
        xm_full_m = probs[:, 2:4]
        y_m = probs[:, 4:6].rearrange("p b (i n) -> p b i n", i=NT)
        xn_m = xn_flat.rearrange("p (t n) -> p t n", t=CT)
        xmT_m = qk_split[:].rearrange("p c a f n -> p (c a f n)").rearrange("p (a f n) -> p a f n", a=2, f=NF)
        stats_m = sb("stats_m", [P, CT, 6])
        mv_m = sb("mv_m", [P, CT, 2])
        rstd_m = sb("rstd_m", [P, CT])
        half_power = sb("half_power", [P, CT])

        q_dram = nc.dram_tensor("q_dram", (2, 2, P, NF * T), fp32, kind="Internal").ap()
        k_dram = nc.dram_tensor("k_dram", (2, 2, P, NF * T), fp32, kind="Internal").ap()
        gate_dram = nc.dram_tensor("gate_dram", (B, 2 * D), fp32, kind="Internal").ap()
        mask_dram = nc.dram_tensor("mask_dram", (B, T), fp32, kind="Internal").ap()

        s_bank = [bank(f"s_bank{i}") for i in range(3)]
        st_bank = [bank(f"st_bank{i}") for i in range(2)]
        o_bank = bank("o_bank")
        g_bank = [bank(f"g_bank{i}") for i in range(2)]

        y_bank = [o_bank, s_bank[2]]

        vec_loaded = sem("vec_loaded")
        late_loaded = sem("late_loaded")
        x_loaded = [sem(f"x_loaded{i}") for i in range(4)]
        wa_loaded = sem("wa_loaded")
        wa_high, wa_split = sem("wa_high"), sem("wa_split")
        wm_loaded = sem("wm_loaded")
        w1_high, w1_split = sem("w1_high"), sem("w1_split")
        w2_high, w2_split = sem("w2_high"), sem("w2_split")
        bias_loaded = sem("bias_loaded")
        gate_loaded = [sem(f"gate_loaded{i}") for i in range(2)]
        ones_set = sem("ones_set")
        rows_set = [sem(f"rows_set{i}") for i in range(2)]
        vones_set = sem("vones_set")
        chain = sem("chain")
        expneg = sem("expneg")
        silu_ready = sem("silu_ready")
        mods_ready = sem("mods_ready")
        bv_spread = sem("bv_spread")
        setup_done = sem("setup_done")
        gates_ready = sem("gates_ready")
        gates_stored = sem("gates_stored")
        maskf_ready = sem("maskf_ready")
        mask_stored = sem("mask_stored")
        stats_part = sem("stats_part")
        power_set = sem("power_set")
        sp_passed, dve_passed, pool_passed = sem("sp_passed"), sem("dve_passed"), sem("pool_passed")
        var_shifted = sem("var_shifted")
        m_shifted = sem("m_shifted")
        mv_ready = sem("mv_ready")
        rstd_ready = sem("rstd_ready")
        xn_ready = sem("xn_ready")
        xT_ready = sem("xT_ready")
        xm_high = sem("xm_high")
        xmT_ready = sem("xmT_ready")
        q_ready = sem("q_ready")
        k_ready = sem("k_ready")
        v_ready = sem("v_ready")
        q_hi = sem("q_hi")
        k_hi = sem("k_hi")
        q_lo = sem("q_lo")
        k_lo = sem("k_lo")
        v_copied = sem("v_copied")
        q_stored = sem("q_stored")
        k_stored = sem("k_stored")
        stack_loaded = [sem(f"stack_loaded{i}") for i in range(2)]
        mask_loaded = [sem(f"mask_loaded{i}") for i in range(2)]
        max_loaded = [sem(f"max_loaded{i}") for i in range(2)]
        s_ready = sem("s_ready")
        max_done = sem("max_done")
        max_joined = sem("max_joined")
        negmax_hi = sem("negmax_hi")
        negmax_ready = sem("negmax_ready")
        negmaxT_ready = sem("negmaxT_ready")
        negmaxT_copied = sem("negmaxT_copied")
        st_ready = sem("st_ready")
        exp_done = sem("exp_done")
        pv_done = sem("pv_done")
        o_copied = sem("o_copied")
        oT_ready = sem("oT_ready")
        rsum_ready = sem("rsum_ready")
        attn_ready = sem("attn_ready")
        attnT_ready = sem("attnT_ready")
        attnT_hi = sem("attnT_hi")
        attnT_lo = sem("attnT_lo")
        proj_ready = sem("proj_ready")
        y_copied = sem("y_copied")
        y_gated = sem("y_gated")
        x_added = sem("x_added")
        m_stats = sem("m_stats")
        m_mv = sem("m_mv")
        m_rstd = sem("m_rstd")
        m_xn = sem("m_xn")
        m_xT = sem("m_xT")
        m_xhigh = sem("m_xhigh")
        m_xmT = sem("m_xmT")
        m_h = sem("m_h")
        m_gelu = sem("m_gelu")
        m_hhigh = sem("m_hhigh")
        m_hT = sem("m_hT")
        m_y = sem("m_y")
        m_ycopied = sem("m_ycopied")
        m_added = sem("m_added")
        out_stored = sem("out_stored")

        block = ctx.enter_context(nc.Block())
        NCH = B * T // CH
        AHEAD = 2
        ATTN_END, MLP_END = B + 3, NCH
        GATE_AT = ROWS_IN.index("gate_attn") * D
        VEC_LOADS, LATE_LOADS, STACK_LOADS = 4, 8, 8
        X_PARTS = (0, 1, 4, 8, B)
        EARLY = 2 * D

        def tab(layer, kind, f, b):
            at = b.count(1, (kind * NF + f) * B)
            return table[layer][:, bass.ds(0 if at is None else at, 1)]

        def xrows(b, tiles, first=0):
            at = b.count(NT * D, first * D)
            return x_sb[:, bass.ds(0 if at is None else at, tiles * D)]

        def in_layer(layer, b):
            return b - (-B * layer)

        @block.sync
        def _(sp):
            def row(name):
                at = ROWS_IN.index(name)
                return rows_in[at:at + 1, :]

            xt = x_in.rearrange("(t p) d -> p t d", p=P)

            def load_x(i):
                at = slice(X_PARTS[i] * NT, X_PARTS[i + 1] * NT)
                sp.dma_start(x_sb[:].rearrange("p (t d) -> p t d", d=D)[:, at], xt[:, at, :])\
                    .then_inc(x_loaded[i], 16)

            for dst, src in [(cond, cond_in), (cols[:], cols_in)]:
                sp.dma_start(dst, src).then_inc(vec_loaded, 16)
            load_x(0)
            for dst, src in [(ada0[:, :, 0:EARLY], ada0_in[:, :, 0:EARLY]), (ident[:], ident_in)]:
                sp.dma_start(dst, src).then_inc(vec_loaded, 16)
            sp.dma_start(wa_raw[0], wa_in[0]).then_inc(wa_loaded, 16)
            load_x(1)
            for dst, src in [(ada0[:, :, EARLY:], ada0_in[:, :, EARLY:]),
                             (gates, rows_in.rearrange("r n -> (r n)")[GATE_AT:].unsqueeze(0)
                              .to_broadcast((B, 2 * D))), (mask_int, mask_in), (tri, tri_in), (ada1, ada1_in), (wo_raw, wa_in[1][:, :, 3 * D:]),
                             (bias_rows[:, 0], row("bproj").to_broadcast((P, D))),
                             (bias_rows[:, 1], row("bo").to_broadcast((P, D)))]:
                sp.dma_start(dst, src).then_inc(late_loaded, 16)
            def constant_rows(layer, stack, half):
                sp.wait_ge(ones_set, 2 * (layer + 1))
                flat = stack[:].rearrange("p a s n -> p (a s n)").bitcast(fp32)
                n = flat.shape[1] // 2
                at, each = slice(half * n, (half + 1) * n), n // ones.shape[1]
                for p in (0, 64):
                    if stack is q_stack:
                        rows = [(ROW_MASK, 1, ones)]
                    else:
                        rows = [(ROW_MAX, 2, ones)] + [(ROW_MASK, 1, zeros)] * (layer == 0)
                    for row, count, src in rows:
                        sp.dma_start(flat[p + row:p + row + count, at], src[0:count * each].bitcast(fp32))\
                            .then_inc(rows_set[half], 16)

            for half in range(2):
                for stack in (q_stack, k_stack):
                    constant_rows(0, stack, half)

            def store_tables():
                sp.wait_ge(gates_ready, 1)
                sp.dma_start(gate_dram, gates).then_inc(gates_stored, 16)
                sp.wait_ge(maskf_ready, 1)
                sp.dma_start(mask_dram, maskf.bitcast(fp32)).then_inc(mask_stored, 16)

            def load_gates(b, kind):
                at = b.count(1)
                sp.dma_start(gate_rows[:, b.mod(2)], gate_dram[bass.ds(0 if at is None else at, 1),
                                                               kind * D:(kind + 1) * D].to_broadcast((P, D)))\
                    .then_inc(gate_loaded[b.mod(2)], 16)

            def when(sem, value):
                wait_apart(sp, sem, value, sp_passed)

            def step(layer, t):
                c, a = t - 3, t - 1
                if c.within(B):
                    g = in_layer(layer, c)
                    when(negmaxT_copied, g.count(1, 1))
                    for p, first in ((0, 0), (64, 16)):
                        sp.dma_start(q_stack[p + ROW_MAX:p + ROW_MAX + 2, g.mod(SBUFS)].bitcast(fp32),
                                     negmaxT[first:first + 16].bitcast(fp32))\
                            .then_inc(max_loaded[g.mod(2)], 16)
                    if layer == 0:
                        when(x_added, c.count(1, -1))
                        load_gates(c, 0)
                if a.within(B):
                    g = in_layer(layer, a)
                    par = g.mod(2)
                    when(stack_loaded[par], g.half().count(16 * STACK_LOADS))
                    when(q_lo, g.count(1, 1))
                    sp.dma_start(q_dram[par].rearrange("a p n -> p a n"),
                                 q_split[:].bitcast(fp32).rearrange("p a f n -> p a (f n)")).then_inc(q_stored, 16)
                    when(k_lo, g.count(1, 1))
                    sp.dma_start(k_dram[par].rearrange("a p n -> p a n"),
                                 k_split[:].bitcast(fp32).rearrange("p a f n -> p a (f n)")).then_inc(k_stored, 16)
                    when(st_ready, g.count(H, H - SBUFS * H))
                    if layer == 1 and a.reg is None and a.const == 0:
                        sp.wait_ge(m_h, NM * NCH)
                        constant_rows(1, q_stack, 0)
                    when(q_stored, g.count(16, 16))
                    for half in (0, 1):
                        src = q_dram[par].rearrange("a (h d i) n -> h a d (i n)", h=2, d=HD)[half]
                        dst = q_stack[64 * half:64 * half + 3 * HD, g.mod(SBUFS)].bitcast(fp32)\
                            .rearrange("p s n -> p (s n)")
                        sp.dma_start(dst[0:2 * HD], src).then_inc(stack_loaded[par], 16)
                        sp.dma_start(dst[2 * HD:3 * HD], src[0]).then_inc(stack_loaded[par], 16)
                    when(k_stored, g.count(16, 16))
                    if layer == 1 and a.reg is None and a.const == 0:
                        sp.wait_ge(m_y, 2 * NCH - 1)
                        constant_rows(1, k_stack, 0)
                    for half in (0, 1):
                        src = k_dram[par].rearrange("a (h d i) n -> h a d (i n)", h=2, d=HD)[half]
                        dst = k_stack[64 * half:64 * half + 3 * HD, g.mod(SBUFS)].bitcast(fp32)\
                            .rearrange("p s n -> p (s n)")
                        sp.dma_start(dst[0:HD], src[0]).then_inc(stack_loaded[par], 16)
                        sp.dma_start(dst[HD:3 * HD], src).then_inc(stack_loaded[par], 16)
                    if layer == 1:
                        at = a.count(1)
                        row = mask_dram[bass.ds(0 if at is None else at, 1), :].unsqueeze(1)\
                            .to_broadcast((1, SLOTS, T))
                        for p in (0, 64):
                            sp.dma_start(k_stack[p + ROW_MASK:p + ROW_MASK + 1, g.mod(SBUFS)].bitcast(fp32), row)\
                                .then_inc(mask_loaded[par], 16)

            def mlp_gates(eng):
                yield Step(0)
                yield Step(1)
                with eng.Fori(0, NCH - 2) as i:
                    yield Step(2, i, 1)

            for layer in range(LAYERS):
                for t in steps(sp, B, AHEAD * layer, 4, 5, 4):
                    if layer == 0 and t.reg is None and t.const == 2:
                        load_x(2)
                    if layer == 0 and t.reg is None and t.const == 3:
                        load_x(3)
                        store_tables()
                        sp.wait_ge(mods_ready, 3)
                        sp.dma_start(w1_raw, w1_in[0]).then_inc(wm_loaded, 16)
                        sp.wait_ge(mask_stored, 16)
                        sp.wait_ge(gates_stored, 16)
                    step(layer, t)
                    if layer == 0 and t.reg is None and t.const == 3:
                        sp.dma_start(w2_raw, w2_in[0]).then_inc(wm_loaded, 16)
                if layer == 0:
                    sp.wait_ge(y_copied, B)
                    sp.dma_start(bias_rows[:, 0], row("b2_0").to_broadcast((P, D))).then_inc(bias_loaded, 16)
                    sp.wait_ge(o_copied, NG * B)
                    sp.dma_start(wa_raw[1], wa_in[1]).then_inc(wa_loaded, 16)
                    for c in mlp_gates(sp):
                        for i in range(2):
                            b = Step(c.const * 2 + i, c.reg, c.stride * 2)
                            if c.reg is None and c.const == 0:
                                sp.wait_ge(x_added, B - 1 + i)
                            else:
                                when(m_added, b.count(1, -1))
                            load_gates(b, 1)
                        if c.reg is None and c.const == 1:
                            sp.wait_ge(w1_split, NM)
                            sp.wait_ge(w2_split, NM)
                            sp.dma_start(w1_raw, w1_in[1]).then_inc(wm_loaded, 16)
                            sp.dma_start(w2_raw, w2_in[1]).then_inc(wm_loaded, 16)
                    for k in range(AHEAD):
                        step(1, Step(k))
                    sp.wait_ge(m_y, 2 * NCH)
                    for stack in (q_stack, k_stack):
                        constant_rows(1, stack, 1)
                    sp.wait_ge(m_ycopied, 2 * NCH)
                    sp.dma_start(bias_rows[:, 0], row("b2_1").to_broadcast((P, D))).then_inc(bias_loaded, 16)
            with sp.Fori(0, NCH) as i:
                when(m_added, i * 2 + (2 * NCH + 2))
                sp.dma_start(out.rearrange("(c t p) d -> p c t d", p=P, t=CT)[:, bass.ds(i, 1)].squeeze(1),
                             x_sb[:, bass.ds(i * (CT * D), CT * D)].rearrange("p (t d) -> p t d", d=D))\
                    .then_inc(out_stored, 16)
            sp.wait_ge(out_stored, 16 * NCH)

        @block.tensor
        def _(pe):
            mm, transpose = nc.tensor.matmul, nc.tensor.transpose

            pe.wait_ge(vec_loaded, 16 * VEC_LOADS)
            pe.wait_ge(silu_ready, 1)

            def columns(bank, at, weights, first, rows):
                for f in range(NF):
                    last = mm(bank[:, at * B:(at + 1) * B], weights[:, f, first:first + P], rows[:, f],
                              start=(f == 0), stop=(f == NF - 1))
                return last

            for j in range(2 * NF):
                last = columns(g_bank[0], j, ada0, j * P, silu)
            last.then_inc(mods_ready, 1)

            def set_up_columns():
                pe.wait_ge(late_loaded, 16 * LATE_LOADS)
                for j in range(2 * NF):
                    columns(s_bank[2], j, ada0, COLUMN_PARTS[2] * D + j * P, silu)
                for j in range(4 * NF):
                    last = columns(s_bank[2], 2 * NF + j, ada1, j * P, cond)
                last.then_inc(mods_ready, 1)

            def set_up_rows():
                for n, part in enumerate(GATE_PARTS):
                    for f in range(NF):
                        mm(st_bank[0][0:B, n * D:(n + 1) * D], silu[:, f], ada0[:, f, part * D:(part + 1) * D],
                           start=(f == 0), stop=(f == NF - 1))
                pe.wait_ge(bv_spread, 1)
                for f in range(NF):
                    last = mm(st_bank[1][:, 0:D], bv_wide[:, f], wo_raw[:, f], start=(f == 0), stop=(f == NF - 1))
                last.then_inc(mods_ready, 1)

            TERMS = [(0, 0), (1, 0), (0, 1)]

            def product(dst, weights, rows, f, tiles):
                for n, (i, j) in enumerate(TERMS):
                    last = mm(dst, weights[i], rows[j], start=(f == 0 and n == 0),
                              stop=(f == tiles - 1 and n == len(TERMS) - 1))
                return last

            USES = [("q", 1, 1, q_lo, 1), ("negmaxT", 0, 3, negmaxT_copied, 1), ("k", 0, 1, k_lo, 1),
                    ("v", 1, 1, v_copied, 1), ("oT0", 0, 4, attn_ready, 2), ("oT1", 1, 4, attn_ready, 2),
                    ("attnT", 0, 4, attnT_lo, 1), ("xT", 1, 0, xm_high, 1), ("proj", 0, 4, y_copied, 1)]

            BANK_OF = {u[0]: u[1] for u in USES}

            def take(layer, t, name):
                at = [u[0] for u in USES].index(name)
                which = USES[at][1]
                for back in range(1, 6 * len(USES)):
                    ago, pos = divmod(at - back, len(USES))
                    user, its, behind, emptied, each = USES[pos]
                    when = t - (behind - ago)
                    if its == which and when.within(B):
                        g = in_layer(layer, when)
                        pe.wait_ge(emptied, g.count(each, 1 if user == "oT0" else each))
                        return g_bank[which]
                return g_bank[which]

            def diagonal(bank):
                return bank[:].rearrange("p (i n) -> p i n", n=P)[:, 0:3:2]

            def scores(layer, g, h):
                p, blk = head_place(h)
                q, k = q_stack[p:p + ROW_MAX, g.mod(SBUFS), blk], k_stack[p:p + ROW_MAX, g.mod(SBUFS), blk]
                if h == 0:
                    pe.wait_ge(stack_loaded[g.mod(2)], g.half().count(16 * STACK_LOADS, 16 * STACK_LOADS))
                    if layer == 1:
                        first = B // 2 * 32
                        pe.wait_ge(mask_loaded[g.mod(2)], g.half().count(32, 32 - first))
                wait(pe, max_done, g.count(H, h - S_AGO[h] + 1))
                bank = s_bank[S_BANK[h]]
                if layer == 0:
                    mm(bank[:, P:3 * P], q[:, P:T], k, start=True, stop=False)
                    mm(bank[:, 0:P], q[:, 0:P], k[:, 0:P], start=False, stop=False)
                    last = mm(diagonal(bank), ident16[:], tri16[:].unsqueeze(1).to_broadcast((P, 2, P)),
                              start=False, stop=True)
                else:
                    for i in range(NT):
                        last = mm(bank[:, i * T:(i + 1) * T], q[:, i * P:(i + 1) * P], k, start=True, stop=True)
                last.then_inc(s_ready, 1)

            def scoresT(layer, g, h):
                p, blk = head_place(h)
                q, k = q_stack[p:p + ROWS, g.mod(SBUFS), blk], k_stack[p:p + ROWS, g.mod(SBUFS), blk]
                if h == 0:
                    pe.wait_ge(max_loaded[g.mod(2)], g.half().count(32, 32))
                wait(pe, exp_done, g.count(H, h - 1))
                bank = st_bank[h % 2]
                if layer == 0:
                    mm(bank[:, 0:T], k[:, 0:P], q, start=True, stop=False)
                    mm(bank[:, 2 * P:3 * P], k[:, P:T], q[:, P:T], start=False, stop=False)
                    last = mm(diagonal(bank), tri16[:], ident16[:].unsqueeze(1).to_broadcast((P, 2, P)),
                              start=False, stop=True)
                else:
                    for i in range(NT):
                        last = mm(bank[:, i * T:(i + 1) * T], k[:, i * P:(i + 1) * P], q, start=True, stop=True)
                last.then_inc(st_ready, 1)

            def attend(layer, g, r):
                pe.wait_ge(exp_done, g.count(H, GROUP * (r + 1)))
                if r == 0:
                    pe.wait_ge(v_copied, g.count(1, 1))
                wait(pe, o_copied, g.count(NG, r))
                first = P if layer == 0 else 0
                for kt in range(NT):
                    for j in range(GROUP):
                        h = GROUP * r + j
                        lo = first if kt else 0
                        last = mm(o_bank[32 * j:32 * j + 32, lo:T], v_sb[:, g.mod(SBUFS), kt, h, :],
                                  probs[:, h % 8, kt * T:kt * T + T - lo], start=(kt == 0), stop=(kt == NT - 1),
                                  tile_position=(0, 32 * j), skip_group_check=True)
                last.then_inc(pv_done, 1)

            def step(layer, t):
                n, a, b, c, d = (t - k for k in range(5))
                gn, ga, gb, gc, gd = (in_layer(layer, s) for s in (n, a, b, c, d))
                for s in range(H):
                    if b.within(B):
                        scores(layer, gb, s)
                    if s < LAG and d.within(B):
                        scoresT(layer, gd, s + H - LAG)
                    if s >= LAG and c.within(B):
                        scoresT(layer, gc, s - LAG)
                    if s == SLOT["xT"] and n.within(B):
                        pe.wait_ge(xn_ready, gn.count(1, 1))
                        bank = take(layer, t, "xT")
                        for f in range(NF):
                            for i in range(NT):
                                last = transpose(bank[:, f * T + i * P:f * T + (i + 1) * P],
                                                 xn[:, gn.mod(2), i, f * P:(f + 1) * P], ident[:])
                        last.then_inc(xT_ready, 1)
                    if s == SLOT["negmaxT"] and c.within(B):
                        pe.wait_ge(negmax_ready, gc.count(1, 1))
                        bank = take(layer, t, "negmaxT")
                        for i in range(NT):
                            src = negmax[:, gc.mod(2), i].bitcast(fp32).rearrange("p a b s -> p (a b s)")
                            last = transpose(bank[0:32, i * P:(i + 1) * P], src, ident[:])
                        last.then_inc(negmaxT_ready, 1)
                    for name, first, ready in (("q", 0, q_ready), ("k", D, k_ready)):
                        if s in SLOT[name] and a.within(B):
                            m = SLOT[name].index(s)
                            if m == 0:
                                bank = take(layer, t, name)
                                if name == "q":
                                    pe.wait_ge(xmT_ready, ga.count(1, 1))
                                    pe.wait_ge(wa_split, 2 * layer + 1)
                            last = project(g_bank[BANK_OF[name]], ga, first, m)
                            if m == NF - 1:
                                last.then_inc(ready, 1)
                    if s in SLOT["v"] and a.within(B):
                        i = SLOT["v"].index(s)
                        if i == 0:
                            take(layer, t, "v")
                        bank = g_bank[BANK_OF["v"]]
                        for f in range(NF):
                            last = product(bank[:, i * D:(i + 1) * D],
                                           [xmT[:, ga.mod(2), e, f, i * P:(i + 1) * P] for e in range(2)],
                                           [wa[:, e, f, 2 * D:3 * D] for e in range(2)], f, NF)
                        if i == NT - 1:
                            last.then_inc(v_ready, 1)
                    if s in SLOT["oT"] and d.within(B):
                        i = SLOT["oT"].index(s)
                        if i == 0:
                            pe.wait_ge(o_copied, gd.count(NG, NG))
                        bank = take(layer, t, f"oT{i}")
                        for r in range(NG):
                            last = transpose(bank[:, r * P:(r + 1) * P], o_sb[:, gd.mod(2), r, i * P:(i + 1) * P],
                                             ident[:])
                        last.then_inc(oT_ready, 1)
                    if s == SLOT["attnT"] and d.within(B):
                        pe.wait_ge(attn_ready, gd.count(2, 2))
                        bank = take(layer, t, "attnT")
                        for f in range(NF):
                            for i in range(NT):
                                last = transpose(bank[:, f * T + i * P:f * T + (i + 1) * P],
                                                 attn[:, i, f * P:(f + 1) * P], ident[:])
                        last.then_inc(attnT_ready, 1)
                    if s in SLOT["proj"] and d.within(B):
                        i = SLOT["proj"].index(s)
                        if i == 0:
                            pe.wait_ge(attnT_lo, gd.count(1, 1))
                            take(layer, t, "proj")
                        bank = g_bank[BANK_OF["proj"]]
                        for f in range(NF):
                            last = product(bank[:, i * D:(i + 1) * D],
                                           [attnT[:, e, f, i * P:(i + 1) * P] for e in range(2)],
                                           [wa[:, e, f, 3 * D:4 * D] for e in range(2)], f, NF)
                        if i == NT - 1:
                            last.then_inc(proj_ready, 1)
                    if s in PV_SLOT:
                        r = PV_SLOT.index(s)
                        g, on = (gc, c) if LAG + 5 + GROUP * r < H else (gd, d)
                        if on.within(B):
                            attend(layer, g, r)
                    if s == SLOT["xT"] and t.reg is None and t.const == ATTN_END:
                        chunk_transposes(layer, Step(0))

            def project(bank, g, first, m):
                at = first + m * P
                for f in range(NF):
                    last = product(bank[:, m * T:(m + 1) * T], [wa[:, e, f, at:at + P] for e in range(2)],
                                   [xmT[:, g.mod(2), e, f, :] for e in range(2)], f, NF)
                return last

            def chunk_transposes(layer, a):
                ga = a - (-NCH * layer)
                pe.wait_ge(m_xn, ga.count(1, 1))
                for f in range(NF):
                    if a.reg is None and a.const == 0:
                        pe.wait_ge(max_done, H * B * (layer + 1))
                    wait(pe, m_xhigh, ga.count(2, f - 1))
                    for i in range(CT):
                        last = transpose(s_bank[f][:, i * P:(i + 1) * P], xn_m[:, i, f * P:(f + 1) * P], ident[:])
                    last.then_inc(m_xT, 1)

            def mlp_step(layer, t):
                a, b = t, t - 1
                gb = b - (-NCH * layer)
                first = b.reg is None and b.const == 0
                ahead = layer == 0 and t.reg is None and t.const == MLP_END

                pe.wait_ge(m_xmT, gb.count(2, 2))
                for m in range(NM):
                    wait(pe, m_gelu, gb.count(NM, m - 1))
                    if first:
                        pe.wait_ge(w1_split, NM * layer + m + 1)
                    for f in range(NF):
                        last = product(st_bank[m % 2][:, :], [w1[:, e, f, m * P:(m + 1) * P] for e in range(2)],
                                       [xmT_m[:, e, f, :] for e in range(2)], f, NF)
                    last.then_inc(m_h, 1)
                if a.within(NCH):
                    chunk_transposes(layer, a)
                if ahead:
                    step(1, Step(0))
                for i in range(2):
                    wait(pe, m_ycopied, gb.count(2, i - 1))
                    for k in range(NT):
                        for m in range(NM):
                            if i == 0 and k == 0:
                                pe.wait_ge(m_hT, gb.count(NM, m + 1))
                                if first:
                                    pe.wait_ge(w2_split, NM * layer + m + 1)
                            last = product(y_bank[i][:, k * D:(k + 1) * D],
                                           [hT[:, i, e, m, k * P:(k + 1) * P] for e in range(2)],
                                           [w2[:, e, m, :] for e in range(2)], m, NM)
                    last.then_inc(m_y, 1)
                    if ahead and i == 0:
                        step(1, Step(1))

            for layer in range(LAYERS):
                for t in steps(pe, B, AHEAD * layer, 4, 5, 4):
                    if layer == 0 and t.reg is None and t.const in (1, 3):
                        pe.wait_ge(setup_done, t.const)
                    if t.reg is None and t.const == 2:
                        if layer == 0:
                            set_up_columns()
                            pe.wait_ge(setup_done, 2)
                        pe.wait_ge(rows_set[0], 96 + 64 * layer)
                        wait(pe, m_ycopied, 2 * NCH * layer or None)
                    if t.reg is None and t.const == 3:
                        pe.wait_ge(rows_set[1], 96 + 64 * layer)
                        pe.wait_ge(vones_set, layer + 1)
                    step(layer, t)
                    if layer == 0 and t.reg is None and t.const == 2:
                        set_up_rows()
                for t in steps(pe, NCH, 1, 2, 2, 2):
                    mlp_step(layer, t)

        @block.scalar
        def _(act):
            activation = nc.scalar.activation
            act.wait_ge(vec_loaded, 16 * VEC_LOADS)
            activation(sig, cond, ACT.Exp, scale=-1.0).then_inc(expneg, 1)
            act.wait_ge(setup_done, 1)
            cq = COLS["bqk"][0]

            def step(layer, t):
                n, a, c, d = t, t - 1, t - 3, t - 4
                gn, ga, gc, gd = (in_layer(layer, s) for s in (n, a, c, d))

                def exponentials(g, h):
                    act.wait_ge(st_ready, g.count(H, h + 1))
                    wait(act, pv_done, g.count(NG, h // GROUP - 1))
                    n = 3 * P if layer == 0 else 4 * P
                    activation(probs[:, h % 8, 0:n], st_bank[h % 2][:, 0:n], ACT.Exp, scale=SCALE)\
                        .then_inc(exp_done, 1)

                def outputs(g, r):
                    act.wait_ge(pv_done, g.count(NG, r + 1))
                    if r == 0:
                        wait(act, oT_ready, g.count(2, -2))
                    activation(o_sb[:, g.mod(2), r, :], o_bank[:, 0:T], ACT.Copy).then_inc(o_copied, 1)

                def high(ready, done, stored, bank, split, first):
                    act.wait_ge(ready, ga.count(1, 1))
                    wait(act, stored, ga.count(16))
                    if layer == 0:
                        activation(split[:, 0], bank[:].rearrange("p (f n) -> p f n", f=NF), ACT.Copy)\
                            .then_inc(done, 1)
                    else:
                        for f in range(NF):
                            last = activation(split[:, 0, f], bank[:, f * T:(f + 1) * T], ACT.Identity,
                                              bias=cols[:, cq + first + f:cq + first + f + 1])
                        last.then_inc(done, 1)

                for s in range(H):
                    if s < LAG and d.within(B):
                        exponentials(gd, s + H - LAG)
                    if s >= LAG and c.within(B):
                        exponentials(gc, s - LAG)
                    if s == SLOT["negmaxT"] and c.within(B):
                        act.wait_ge(negmaxT_ready, gc.count(1, 1))
                        last_batch = gc - 1
                        wait(act, max_loaded[last_batch.mod(2)], last_batch.half().count(32, 32)
                             if c.reg is not None or c.const + layer else None)
                        activation(negmaxT[:], g_bank[0][0:32, 0:T], ACT.Copy).then_inc(negmaxT_copied, 1)
                    if s == SLOT["q"][1] and a.within(B):
                        high(q_ready, q_hi, q_stored, g_bank[1], q_split, 0)
                    if s == SLOT["k"][1] and a.within(B):
                        high(k_ready, k_hi, k_stored, g_bank[0], k_split, NF)
                    if s == SLOT["v"][1] and a.within(B):
                        act.wait_ge(v_ready, ga.count(1, 1))
                        wait(act, pv_done, ga.count(NG, NG - SBUFS * NG))
                        activation(v_sb[:, ga.mod(SBUFS), :, :, 0:HD],
                                   g_bank[1][:].rearrange("p (i h d) -> p i h d", i=NT, h=H), ACT.Copy)\
                            .then_inc(v_copied, 1)
                    if s == SLOT["attnT"] and d.within(B):
                        act.wait_ge(attnT_ready, gd.count(1, 1))
                        wait(act, proj_ready, gd.count(1))
                        activation(attnT[:, 0], g_bank[0][:].rearrange("p (f n) -> p f n", f=NF), ACT.Copy)\
                            .then_inc(attnT_hi, 1)
                    if s in (SLOT["xT"], SLOT["xT"] + 1) and n.within(B):
                        f = s - SLOT["xT"]
                        if f == 0:
                            act.wait_ge(xT_ready, gn.count(1, 1))
                            wait(act, v_ready, gn.count(1, -1))
                            wait(act, xmT_ready, gn.count(1))
                        for dst in (xm_full, xmT[:, gn.mod(2), 0]):
                            last = activation(dst[:, f], g_bank[1][:, f * T:(f + 1) * T], ACT.Identity,
                                              scale=tab(layer, A1, f, n), bias=tab(layer, B1, f, n))
                        if f == NF - 1:
                            last.then_inc(xm_high, 1)
                    if s in PV_SLOT:
                        r = PV_SLOT.index(s)
                        g, on = (gc, c) if LAG + 5 + GROUP * r < H else (gd, d)
                        if on.within(B):
                            outputs(g, r)
                    if s == SLOT["xT"] and t.reg is None and t.const == ATTN_END:
                        chunk_modulated(layer, Step(0))

            def chunk_modulated(layer, a):
                ga = a - (-NCH * layer)
                for f in range(NF):
                    act.wait_ge(m_xT, ga.count(2, f + 1))
                    wait(act, m_xmT, ga.count(2, f - 1))
                    if a.reg is None and a.const == 0 and f == 0:
                        act.wait_ge(pv_done, NG * B * (layer + 1))
                        act.wait_ge(q_stored, 16 * B * (layer + 1))
                        act.wait_ge(k_stored, 16 * B * (layer + 1))
                    for dst in (xm_full_m[:, f], xmT_m[:, 0, f]):
                        for k in range(2):
                            at = slice(k * T, (k + 1) * T)
                            batch = Step(a.const * 2 + k, a.reg, a.stride * 2)
                            last = activation(dst[:, at], s_bank[f][:, at], ACT.Identity,
                                              scale=tab(layer, A2, f, batch), bias=tab(layer, B2, f, batch))
                    last.then_inc(m_xhigh, 1)

            def mlp_step(layer, t):
                a, b = t, t - 1
                gb = b - (-NCH * layer)
                if b.within(NCH):
                    cb = COLS[f"b1_{layer}"][0]
                    for m in range(NM):
                        act.wait_ge(m_h, gb.count(NM, m + 1))
                        wait(act, m_hT, gb.count(NM, m - 1))
                        activation(h_full[:, m % 2], st_bank[m % 2][:, :], ACT.Gelu, bias=cols[:, cb + m:cb + m + 1])\
                            .then_inc(m_gelu, 1)
                if a.within(NCH):
                    chunk_modulated(layer, a)
                if layer == 0 and t.reg is None and t.const == 1:
                    act.wait_ge(proj_ready, B)
                    act.wait_ge(wa_loaded, 32)
                    for f in range(NF):
                        activation(wa[:, 0, f], wa_raw[1][:, f], ACT.Copy).then_inc(wa_high, 1)
                if layer == 0 and t.reg is None and t.const == MLP_END:
                    for k in range(AHEAD):
                        step(1, Step(k))

            for layer in range(LAYERS):
                for t in steps(act, B, AHEAD * layer, 4, 5, 4):
                    if t.reg is None and t.const == 3:
                        act.wait_ge(setup_done, 3)
                        act.wait_ge(mask_stored, 16)
                        for half in range(2):
                            act.wait_ge(rows_set[half], 96 + 64 * layer)
                        wait(act, m_added, 2 * NCH * layer or None)
                        wait(act, m_hT, NM * NCH * layer or None)
                    step(layer, t)
                act.wait_ge(st_ready, H * B * (layer + 1))
                act.wait_ge(wm_loaded, 32 * (layer + 1))
                for m in range(NM):
                    at = slice(m * P, (m + 1) * P)
                    activation(w1[:, 0, :, at], w1_raw[:, :, at], ACT.Copy).then_inc(w1_high, 1)
                for m in range(NM):
                    activation(w2[:, 0, m], w2_raw[:, m], ACT.Copy).then_inc(w2_high, 1)
                for t in steps(act, NCH, 1, 2, 2, 2):
                    mlp_step(layer, t)

        @block.vector
        def _(dve):
            v = nc.vector
            links = [0]

            def link(ins):
                links[0] += 1
                ins.then_inc(chain, 1)
                dve.wait_ge(chain, links[0])

            def set_ones():
                v.memset(ones.bitcast(fp32), 1.0).then_inc(ones_set, 1)
                v.memset(zeros.bitcast(fp32), 0.0).then_inc(ones_set, 1)

            def split(dst, src, high, last_high, low):
                v.tensor_copy(dst[0], src).then_inc(high, 1)
                dve.wait_ge(high, last_high)
                v.tensor_tensor(dst[1], src, dst[0], ALU.subtract).then_inc(low, 1)

            def split_attention_weights():
                dve.wait_ge(wa_loaded, 16)
                split([wa[:, e] for e in range(2)], wa_raw[0], wa_high, 1, wa_split)

            def split_w1(layer):
                dve.wait_ge(wm_loaded, 32 * (layer + 1))
                dve.wait_ge(st_ready, B * H * (layer + 1))
                for m in range(NM):
                    at = slice(m * P, (m + 1) * P)
                    dve.wait_ge(w1_high, NM * layer + m + 1)
                    v.tensor_tensor(w1[:, 1, :, at], w1_raw[:, :, at], w1[:, 0, :, at], ALU.subtract)\
                        .then_inc(w1_split, 1)

            def col(name, n, first=0):
                at = COLS[name][0] + first
                return cols[:, at:at + n].unsqueeze(2).to_broadcast((P, n, B))

            def kind(layer, k):
                return table[layer][:, k * NF * B:(k + 1) * NF * B].rearrange("p (f b) -> p f b", f=NF)

            def set_up_first():
                dve.wait_ge(vec_loaded, 16 * VEC_LOADS)
                dve.wait_ge(expneg, 1)
                link(v.tensor_scalar(sig, sig, 1.0, None, ALU.add))
                link(v.reciprocal(sig, sig))
                v.tensor_tensor(silu, sig, cond, ALU.mult).then_inc(silu_ready, 1)
                row_statistics(0, Step(0))
                row_normalise(0, Step(0))
                dve.wait_ge(mods_ready, 1)
                layer0_columns(0, g_bank[0], 0).then_inc(setup_done, 1)

            def layer0_columns(n, bank, at):
                mods = mod0[:, 2 * n * NF:2 * (n + 1) * NF]
                link(v.tensor_tensor(mods, bank[:, at * B:(at + 2 * NF) * B].rearrange("p (j b) -> p j b", b=B),
                                     col("bada", 2 * NF, COLUMN_PARTS[2 * n] * NF), ALU.add))
                shift, scale = mods[:, 0:NF], mods[:, NF:]
                v.scalar_tensor_tensor(out=kind(0, 2 * n), in0=scale, scalar=1.0, in1=col(f"g{n + 1}", NF),
                                       op0=ALU.add, op1=ALU.mult)
                link(v.scalar_tensor_tensor(out=kind(0, 2 * n + 1), in0=scale, scalar=1.0,
                                            in1=col(f"be{n + 1}", NF), op0=ALU.add, op1=ALU.mult))
                return v.tensor_tensor(kind(0, 2 * n + 1), kind(0, 2 * n + 1), shift, ALU.add)

            def set_up_columns():
                c0 = COLS["bv"][0]
                dve.wait_ge(late_loaded, 16 * LATE_LOADS)
                v.tensor_copy(bv_wide, cols[:, c0:c0 + NF].unsqueeze(2).to_broadcast((P, NF, P)))\
                    .then_inc(bv_spread, 1)
                v.tensor_copy(ident16[:], ident[:])
                v.tensor_copy(tri16[:], tri)
                v.tensor_scalar(maskf, mask_int, BIG, None, ALU.mult).then_inc(maskf_ready, 1)
                dve.wait_ge(mods_ready, 2)
                layer0_columns(1, s_bank[2], 0)
                link(v.tensor_tensor(mod1, s_bank[2][:, 2 * NF * B:6 * NF * B].rearrange("p (j b) -> p j b", b=B),
                                     col("bada1", 4 * NF), ALU.add))
                for first, ka, kb in ((0, A1, B1), (2, A2, B2)):
                    v.tensor_scalar(kind(1, ka), mod1[:, first * NF:(first + 1) * NF], 1.0, None, ALU.add)
                    last = v.tensor_copy(kind(1, kb), mod1[:, (first + 1) * NF:(first + 2) * NF])
                last.then_inc(setup_done, 1)

            def set_up_rows():
                dve.wait_ge(mods_ready, 3)
                v.tensor_tensor(gates, st_bank[0][0:B, :], gates, ALU.add).then_inc(gates_ready, 1)
                v.tensor_tensor(bias_rows[:, 1], st_bank[1][:, 0:D], bias_rows[:, 1], ALU.add)\
                    .then_inc(setup_done, 1)

            def statistics(rows, tiles, into, mean_var, part, done, g, used):
                wait(dve, used[0], used[1])
                for i in range(tiles):
                    v.bn_stats(into[:, i, :], rows[:, i * D:(i + 1) * D]).then_inc(part, 1)
                wait_apart(dve, part, g.count(tiles, tiles), dve_passed)
                for i in range(tiles):
                    last = v.bn_aggr(mean_var[:, i, :], into[:, i, :])
                last.then_inc(done, 1)

            def normalise(rows, tiles, dst, mean_var, rs, rdy, done, g):
                dve.wait_ge(rdy, g.count(1, 1))
                for i in tiles:
                    last = v.tensor_scalar(dst[:, i, :], rows[:, i * D:(i + 1) * D], mean_var[:, i, 0:1],
                                           rs[:, i:i + 1], ALU.subtract, ALU.mult)
                if done is not None:
                    last.then_inc(done, 1)

            def low(layer, g, ready, done, bank, split, first):
                dve.wait_ge(ready, g.count(1, 1))
                c = COLS["bqk"][0] + first
                if layer == 0:
                    v.tensor_tensor(split[:, 1], bank[:].rearrange("p (f n) -> p f n", f=NF), split[:, 0],
                                    ALU.subtract).then_inc(done, 1)
                else:
                    for f in range(NF):
                        last = v.scalar_tensor_tensor(out=split[:, 1, f], in0=bank[:, f * T:(f + 1) * T],
                                                      scalar=cols[:, c + f:c + f + 1], in1=split[:, 0, f],
                                                      op0=ALU.add, op1=ALU.subtract)
                    last.then_inc(done, 1)

            def row_statistics(layer, n):
                gn = in_layer(layer, n)
                if n.reg is None:
                    dve.wait_ge(x_loaded[min(n.const, 1)], 16)
                elif layer == 0 and n.const == 4:
                    for i in (2, 3):
                        dve.wait_ge(x_loaded[i], 16)
                if layer:
                    dve.wait_ge(m_added, n.count(1, 1))
                statistics(xrows(n, NT), NT, stats[:, gn.mod(2)], mv[:, gn.mod(2)], stats_part, mv_ready, gn,
                           (xn_ready, gn.count(1, -1)))

            def row_normalise(layer, n):
                gn = in_layer(layer, n)
                wait(dve, xT_ready, gn.count(1, -1))
                if layer and n.reg is None and n.const < 2:
                    dve.wait_ge(m_xT, 2 * NCH)
                normalise(xrows(n, NT), range(NT), xn[:, gn.mod(2)], mv[:, gn.mod(2)], rstd[:, gn.mod(2)],
                          rstd_ready, xn_ready, gn)

            def step(layer, t):
                n, a, b, d = t, t - 1, t - 2, t - 4
                gn, ga, gb, gd = (in_layer(layer, s) for s in (n, a, b, d))
                last_step = t.reg is None and t.const == ATTN_END
                for s in range(H):
                    if b.within(B):
                        if s == 0:
                            wait(dve, negmax_ready, gb.count(1, -1))
                        dve.wait_ge(s_ready, gb.count(H, s + 1))
                        bank = s_bank[S_BANK[s]]
                        if layer == 0:
                            v.reduce_max(maxima[:, gb.mod(2), s, 0:3],
                                         bank[:, 0:3 * P].rearrange("p (i n) -> p i n", n=P), AX.X)\
                                .then_inc(max_done, 1)
                        else:
                            v.reduce_max(maxima[:, gb.mod(2), s, 0:2],
                                         bank[:].rearrange("p (i n) -> p i n", n=T), AX.X).then_inc(max_done, 1)
                    if s == SLOT["q"][1] and a.within(B):
                        low(layer, ga, q_hi, q_lo, g_bank[1], q_split, 0)
                    if s == 3 and n.within(B):
                        row_statistics(layer, n)
                    if s == SLOT["k"][1] and a.within(B):
                        low(layer, ga, k_hi, k_lo, g_bank[0], k_split, NF)
                    if s == 7 and n.within(B):
                        row_normalise(layer, n)
                    if s in SLOT["oT"] and d.within(B):
                        i = SLOT["oT"].index(s)
                        dve.wait_ge(oT_ready, gd.count(2, i + 1))
                        if i == 0:
                            wait(dve, attnT_ready, gd.count(1))
                            if layer == 0 and d.const == 0:
                                dve.wait_ge(gates_stored, 16)
                        o = g_bank[i][:].rearrange("p (h n) -> p h n", n=32)
                        wait(dve, attn_ready, gd.count(2, i))
                        v.reciprocal(rsum[:, i], o[:, :, HD]).then_inc(rsum_ready, 1)
                        dve.wait_ge(rsum_ready, gd.count(2, i + 1))
                        v.tensor_tensor(attn[:, i].rearrange("p (h n) -> p h n", n=HD), o[:, :, 0:HD],
                                        rsum[:, i].unsqueeze(2).to_broadcast((P, H, HD)), ALU.mult)\
                            .then_inc(attn_ready, 1)
                    if s == SLOT["attnT"] and d.within(B):
                        dve.wait_ge(attnT_hi, gd.count(1, 1))
                        v.tensor_tensor(attnT[:, 1], g_bank[0][:].rearrange("p (f n) -> p f n", f=NF), attnT[:, 0],
                                        ALU.subtract).then_inc(attnT_lo, 1)
                    if s == SLOT["proj"][1] and d.within(B):
                        dve.wait_ge(proj_ready, gd.count(1, 1))
                        wait(dve, x_added, gd.count(1))
                        v.tensor_tensor(y_sb[:], g_bank[0][:].rearrange("p (i n) -> p i n", i=NT),
                                        bias_rows[:, layer].unsqueeze(1).to_broadcast((P, NT, D)), ALU.add)\
                            .then_inc(y_copied, 1)
                    if last_step and s == SLOT["k"][1]:
                        chunk_statistics(layer, Step(0))
                    if last_step and s == 7:
                        chunk_normalise(layer, Step(0), range(CT))
                    if last_step and s == SLOT["xT"]:
                        chunk_low(layer, Step(0))
                        split_w1(layer)
                if b.within(B):
                    m = maxima[:, gb.mod(2)]
                    dve.wait_ge(max_done, gb.count(H, H))
                    if layer == 0:
                        v.tensor_tensor(m[:, :, 1], m[:, :, 1], m[:, :, 2], ALU.max).then_inc(max_joined, 1)
                        dve.wait_ge(max_joined, gb.count(1, 1))
                    wait(dve, negmaxT_ready, gb.count(1, -1))
                    for i in range(NT):
                        src = m[:, :, i].rearrange("p (f j e) -> p e j f", f=2, e=2)
                        dst = negmax[:, gb.mod(2), i].rearrange("p e c (j f) -> p e c j f", f=2)
                        last = v.tensor_scalar(dst[:, :, 0], src, -1.0, None, ALU.mult)
                    last.then_inc(negmax_hi, 1)
                    dve.wait_ge(negmax_hi, gb.count(1, 1))
                    for i in range(NT):
                        src = m[:, :, i].rearrange("p (f j e) -> p e j f", f=2, e=2)
                        dst = negmax[:, gb.mod(2), i].rearrange("p e c (j f) -> p e c j f", f=2)
                        for e in range(2):
                            last = v.scalar_tensor_tensor(out=dst[:, e, 1], in0=src[:, e], scalar=-1.0,
                                                          in1=dst[:, e, 0], op0=ALU.mult, op1=ALU.subtract)
                    last.then_inc(negmax_ready, 1)

            def chunk_rows(chunk):
                return xrows(Step(chunk.const * 2, chunk.reg, chunk.stride * 2), CT)

            def chunk_statistics(layer, a):
                ga = a - (-NCH * layer)
                dve.wait_ge(x_added, ga.count(2, 2))
                statistics(chunk_rows(a), CT, stats_m, mv_m, m_stats, m_mv, ga, (m_xn, ga.count(1)))

            def chunk_normalise(layer, a, tiles):
                ga = a - (-NCH * layer)
                if tiles[0] == 0:
                    if a.reg is None and a.const == 0:
                        dve.wait_ge(xT_ready, B * (layer + 1))
                    wait(dve, m_xT, ga.count(2))
                normalise(chunk_rows(a), tiles, xn_m, mv_m, rstd_m, m_rstd, m_xn if tiles[-1] == CT - 1 else None,
                          ga)

            def chunk_low(layer, a):
                ga = a - (-NCH * layer)
                for f in range(NF):
                    dve.wait_ge(m_xhigh, ga.count(2, f + 1))
                    v.tensor_tensor(xmT_m[:, 1, f], xm_full_m[:, f], xmT_m[:, 0, f], ALU.subtract)\
                        .then_inc(m_xmT, 1)

            def mlp_step(layer, t):
                a, b = t, t - 1
                gb = b - (-NCH * layer)
                ahead = layer == 0 and t.reg is None and t.const == MLP_END
                if a.within(NCH):
                    chunk_statistics(layer, a)
                if ahead:
                    row_statistics(1, Step(0))
                for m in range(NM):
                    dve.wait_ge(m_gelu, gb.count(NM, m + 1))
                    if m == 0:
                        wait(dve, m_y, gb.count(2))
                    h = h_full[:, m % 2].rearrange("p (i n) -> p i n", i=2)
                    v.tensor_copy(hT[:, :, 0, m], h).then_inc(m_hhigh, 1)
                    dve.wait_ge(m_hhigh, gb.count(NM, m + 1))
                    v.tensor_tensor(hT[:, :, 1, m], h, hT[:, :, 0, m], ALU.subtract).then_inc(m_hT, 1)
                    if a.within(NCH) and m in (2, 4):
                        chunk_normalise(layer, a, range(m - 2, m))
                    if ahead and m == 3:
                        row_normalise(1, Step(0))
                if a.within(NCH):
                    chunk_low(layer, a)
                for i in range(2):
                    dve.wait_ge(m_y, gb.count(2, i + 1))
                    wait(dve, m_added, gb.count(2, i - 1))
                    if b.reg is None and b.const == 0 and i == 0:
                        dve.wait_ge(bias_loaded, 16 * (layer + 1))
                    v.tensor_tensor(y_m[:, i], y_bank[i][:].rearrange("p (i n) -> p i n", i=NT),
                                    bias_rows[:, 0].unsqueeze(1).to_broadcast((P, NT, D)), ALU.add)\
                        .then_inc(m_ycopied, 1)
                    if ahead and i == 0:
                        step(1, Step(1))
                if layer == 0 and t.reg is None and t.const == 1:
                    dve.wait_ge(proj_ready, B)
                    set_ones()

            set_ones()
            set_up_first()
            for layer in range(LAYERS):
                for t in steps(dve, B, layer + 1, 4, 5, 4):
                    if layer == 0 and t.reg is None and t.const == 1:
                        split_attention_weights()
                    if layer == 0 and t.reg is None and t.const == 2:
                        set_up_columns()
                    step(layer, t)
                    if layer == 0 and t.reg is None and t.const == 2:
                        set_up_rows()
                for t in steps(dve, NCH, 1, 2, 2, 2):
                    mlp_step(layer, t)

        @block.gpsimd
        def _(pool):
            g_ = nc.gpsimd

            g_.memset(half_power[:], -0.5).then_inc(power_set, 1)
            pool.wait_ge(power_set, 1)

            def inverse_deviation(dst, var, tiles, shifted, g, done):
                g_.tensor_scalar(dst, var, EPS, 1.0, ALU.add, ALU.mult).then_inc(shifted, 1)
                pool.wait_ge(shifted, g.count(1, 1))
                g_.tensor_tensor(dst, dst, half_power[:, 0:tiles], ALU.pow).then_inc(done, 1)

            def output(layer, y, rows, gate, copied, done):
                pool.wait_ge(*copied)
                if layer == 0:
                    pool.wait_ge(gate_loaded[gate[0]], gate[1])
                    g_.tensor_tensor(y, y, gate_rows[:, gate[0]].unsqueeze(1).to_broadcast((P, NT, D)), ALU.mult)\
                        .then_inc(y_gated, 1)
                    pool.wait_ge(y_gated, gate[2])
                g_.tensor_tensor(rows.rearrange("p (i n) -> p i n", i=NT), rows.rearrange("p (i n) -> p i n", i=NT),
                                 y, ALU.add).then_inc(done, 1)

            def chunk_deviation(layer, a):
                g = a - (-NCH * layer)
                wait_apart(pool, m_mv, g.count(1, 1), pool_passed)
                inverse_deviation(rstd_m[:], mv_m[:, :, 1], CT, m_shifted, g, m_rstd)

            def row_deviation(layer, n):
                gn = in_layer(layer, n)
                wait_apart(pool, mv_ready, gn.count(1, 1), pool_passed)
                inverse_deviation(rstd[:, gn.mod(2)], mv[:, gn.mod(2), :, 1], NT, var_shifted, gn, rstd_ready)

            def modulated_low(layer, n):
                gn = in_layer(layer, n)
                pool.wait_ge(xm_high, gn.count(1, 1))
                g_.tensor_tensor(xmT[:, gn.mod(2), 1], xm_full[:], xmT[:, gn.mod(2), 0], ALU.subtract)\
                    .then_inc(xmT_ready, 1)

            def step(layer, t):
                n, d = t, t - 4
                gd = in_layer(layer, d)
                if n.within(B):
                    row_deviation(layer, n)
                    modulated_low(layer, n)
                if t.reg is None and t.const == ATTN_END:
                    chunk_deviation(layer, Step(0))
                    for m in range(NM):
                        pool.wait_ge(w2_high, NM * layer + m + 1)
                        g_.tensor_tensor(w2[:, 1, m], w2_raw[:, m], w2[:, 0, m], ALU.subtract).then_inc(w2_split, 1)
                if d.within(B):
                    output(layer, y_sb[:], xrows(d, NT), (gd.mod(2), gd.half().count(16, 16), gd.count(1, 1)),
                           (y_copied, gd.count(1, 1)), x_added)

            def mlp_step(layer, t):
                a, b = t, t - 1
                gb = b - (-NCH * layer)
                ahead = layer == 0 and t.reg is None and t.const == MLP_END
                if a.within(NCH):
                    chunk_deviation(layer, a)
                if ahead:
                    row_deviation(1, Step(0))
                    pool.wait_ge(wa_split, 3)
                    g_.memset(v_sb[:, :, :, :, HD:32], 1.0).then_inc(vones_set, 1)
                    modulated_low(1, Step(0))
                for i in range(2):
                    batch = Step(b.const * 2 + i, b.reg, b.stride * 2)
                    output(layer, y_m[:, i], xrows(batch, NT),
                           (i, b.count(16, 16 * (B // 2) + 16), batch.count(1, B + 1)),
                           (m_ycopied, gb.count(2, i + 1)), m_added)
                    if ahead and i == 0:
                        step(1, Step(1))
                if layer == 0 and t.reg is None and t.const == 1:
                    for f in range(NF):
                        pool.wait_ge(wa_high, 2 + f)
                        g_.tensor_tensor(wa[:, 1, f], wa_raw[1][:, f], wa[:, 0, f], ALU.subtract).then_inc(wa_split, 1)

            g_.memset(v_sb[:, :, :, :, HD:32], 1.0).then_inc(vones_set, 1)
            for layer in range(LAYERS):
                for t in steps(pool, B, AHEAD * layer, 4, 5, 4):
                    step(layer, t)
                for t in steps(pool, NCH, 1, 2, 2, 2):
                    mlp_step(layer, t)


def kernel(**inputs):
    import numpy as np
    import concourse.bacc as bacc
    from concourse.bass_utils import run_bass_kernel_spmd

    a = {k: np.asarray(v) for k, v in inputs.items()}

    def rows(w):
        return np.ascontiguousarray(w.reshape(-1, P, w.shape[1]).transpose(1, 0, 2))

    def columns(v):
        return v.reshape(-1, P).T

    order = np.array([((4 * t + i) * 2 + par) * HD + d
                      for t in range(NF) for par in range(2) for d in range(HD) for i in range(4)])
    wqkv0 = a["L0_cond_Wqkv"]
    q0, k0, v0 = wqkv0[:, 0:D], wqkv0[:, D:2 * D], wqkv0[:, 2 * D:]
    q1, k1, v1 = a["L1_cond_wq"].T, a["L1_cond_wk"].T, a["L1_cond_wv"].T
    vectors = {"g1": a["L0_cond_g1"], "be1": a["L0_cond_be1"], "g2": a["L0_cond_g2"], "be2": a["L0_cond_be2"],
               "b1_0": a["L0_cond_b1"],
               "bada": a["L0_cond_bada"], "bada1": np.concatenate([a["L1_cond_b_adaln1"], a["L1_cond_b_adaln2"]]),
               "bqk": np.concatenate([a["L1_cond_bq"][order], a["L1_cond_bk"][order]]), "bv": a["L1_cond_bv"],
               "b1_1": a["L1_cond_b1"]}
    bada = a["L0_cond_bada"]
    rows_of = {"bproj": a["L0_cond_bproj"], "b2_0": a["L0_cond_b2"], "bo": a["L1_cond_bo"], "b2_1": a["L1_cond_b2"],
               "gate_attn": bada[2 * D:3 * D], "gate_mlp": bada[5 * D:6 * D]}
    mask_words = np.zeros((B, T, 4), np.uint8)
    mask_words[:, :, 0] = a["mask_BxS_bf0"].view(np.uint8)
    arrays = {
        "x_in": a["x"].reshape(B * T, D),
        "cond_in": rows(a["cond_1024"].T),
        "mask_in": mask_words.view(np.int32)[:, :, 0],
        "wa_in": np.stack([rows(np.concatenate([q0[:, order], k0[:, order], v0, a["L0_cond_Wproj"]], axis=1)),
                           rows(np.concatenate([q1[:, order], k1[:, order], v1, a["L1_cond_wo"].T], axis=1))]),
        "w1_in": np.stack([rows(a["L0_cond_W1"]), rows(a["L1_cond_w1"].T)]),
        "w2_in": np.stack([rows(a["L0_cond_W2"]), rows(a["L1_cond_w2"].T)]),
        "ada0_in": rows(a["L0_cond_Wada"]),
        "ada1_in": rows(np.concatenate([a["L1_cond_w_adaln1"].T, a["L1_cond_w_adaln2"].T], axis=1)),
        "cols_in": np.concatenate([columns(vectors[name]) for name in COLS], axis=1),
        "rows_in": np.stack([rows_of[name] for name in ROWS_IN]),
        "ident_in": np.eye(P, dtype=np.float32),
        "tri_in": np.where(np.arange(P)[None, :] > np.arange(P)[:, None], BIG, 0.0).astype(np.float32),
    }
    nc = bacc.Bacc("TRN2", target_bir_lowering=False, num_devices=1)
    args = []
    for name in arrays:
        arrays[name] = np.ascontiguousarray(arrays[name])
        args.append(nc.dram_tensor(name, arrays[name].shape, mybir.dt.from_np(arrays[name].dtype),
                                   kind="ExternalInput").ap())
    out = nc.dram_tensor("out", (B * T, D), mybir.dt.float32, kind="ExternalOutput").ap()
    build(nc, *args, out)
    r = run_bass_kernel_spmd(nc, [arrays], core_ids=[0])
    return r.results[0]["out"].reshape(B, T, D)
```
